# Optimizing a Trainium2 kernel written in Bass

```python
import numpy as np
import jax
import jax.numpy as jnp

def _softmax(x, axis=-1):
    return jax.nn.softmax(x, axis=axis)

def _gelu(x):
    return jax.nn.gelu(x, approximate=True)

def _silu(x):
    return jax.nn.silu(x)

def _sigmoid(x):
    return jax.nn.sigmoid(x)

def _layernorm(x, axis=-1, eps=1e-05):
    m = jnp.mean(x, axis=axis, keepdims=True)
    v = jnp.var(x, axis=axis, keepdims=True)
    return (x - m) / jnp.sqrt(v + eps)

def _scatter_add(tgt, idx, src, axis=0):
    return tgt.at[idx].add(src)

def _segment_sum(src, seg, n):
    return jax.ops.segment_sum(src, seg, n)
kernel_name = 'mk_xattn_ffn_d1_seqx_r8_156796'

def setup_inputs(seed: int=0):
    np.random.seed(seed)
    _w = jnp.asarray

    def _rec_inputs():
        import jax
        import jax.numpy as jnp
        _rk = jax.random.key(seed)
        x = -0.0003929 + 0.9999 * jax.random.normal(jax.random.fold_in(_rk, 1), (8, 128, 256), jnp.float32)
        _lenS = 128 - jax.random.randint(jax.random.fold_in(_rk, 7), (8,), 0, max(1, 128 // 4) + 1, jnp.int32)
        _lenS2 = 128 - jax.random.randint(jax.random.fold_in(_rk, 8), (8,), 0, max(1, 128 // 4) + 1, jnp.int32)
        _ctx_1024P = jax.random.normal(jax.random.fold_in(_rk, 11), (8, 16, 128), jnp.float32)
        _ctx_1024c = jax.random.dirichlet(jax.random.fold_in(_rk, 511), 0.3 * jnp.ones((16,), jnp.float32), (8, 128))
        _ctx_1024t = jnp.einsum('bsk,bkd->bsd', _ctx_1024c, _ctx_1024P)
        _ctx_1024t = _ctx_1024t * jax.lax.rsqrt(jnp.mean(jnp.square(_ctx_1024t)) + 1e-12) * 0.953939
        ctx_1024 = 0.000227908 + 0.99994 * (_ctx_1024t + 0.3 * jax.random.normal(jax.random.fold_in(_rk, 611), (8, 128, 128), jnp.float32))
        return (x, ctx_1024)
    x, ctx_1024 = _rec_inputs()

    def _L0_xattn_setup():
        import jax, jax.numpy as jnp
        import numpy as np
        EPS = 1e-05

        def rmsnorm(x, g, eps=EPS):
            var = jnp.mean(jnp.square(x), axis=-1, keepdims=True)
            return x * jax.lax.rsqrt(var + eps) * g
        key = jax.random.key(seed)
        ks = jax.random.split(key, 8)
        B, Sq, Skv = (2, 512, 64)
        dim, cdim, H, D = (256, 128, 16, 128)
        inner = H * D
        s = lambda f: 1.0 / np.sqrt(f)
        return {'hidden_states': jax.random.normal(ks[0], (B, Sq, dim), jnp.float32), 'encoder_hidden_states': jax.random.normal(ks[1], (B, Skv, cdim), jnp.float32), 'Wq': jax.random.normal(ks[2], (dim, inner), jnp.float32) * s(dim), 'Wk': jax.random.normal(ks[3], (cdim, inner), jnp.float32) * s(cdim), 'Wv': jax.random.normal(ks[4], (cdim, inner), jnp.float32) * s(cdim), 'Wo': jax.random.normal(ks[5], (inner, dim), jnp.float32) * s(inner), 'gq': jnp.ones((D,), jnp.float32), 'gk': jnp.ones((D,), jnp.float32)}
    _L0_xattn_all = _L0_xattn_setup()
    _L0_xattn_in = {k: v for k, v in _L0_xattn_all.items() if k in ('Wq', 'Wk', 'Wv', 'Wo', 'gq', 'gk')}
    del _L0_xattn_all

    def _L0_ffn_setup():
        import jax, jax.numpy as jnp
        import numpy as np
        BLOCK_SIZE = 32
        HIDDEN_SIZE = 256
        MLP_DIM = 2048
        NVFP4_LUT = jnp.array([0.0, 0.5, 1.0, 1.5, 2.0, 3.0, 4.0, 6.0, 0.0, -0.5, -1.0, -1.5, -2.0, -3.0, -4.0, -6.0], dtype=jnp.float32)

        def dequant_nvfp4(W_packed, scales, block=BLOCK_SIZE):
            N = W_packed.shape[0]
            low = W_packed & 15
            high = W_packed >> 4 & 15
            idx = jnp.stack([low, high], axis=-1).reshape(N, -1)
            vals = NVFP4_LUT[idx]
            K = vals.shape[1]
            vals = vals.reshape(N, K // block, block) * scales[:, :, None]
            return vals.reshape(N, K)
        key = jax.random.key(seed)
        ks = jax.random.split(key, 7)
        x = jax.random.normal(ks[0], (4, 32, HIDDEN_SIZE), dtype=jnp.float32)
        gate_W_packed = jax.random.randint(ks[1], (MLP_DIM, HIDDEN_SIZE // 2), 0, 32, dtype=jnp.int32)
        gate_scales = jax.random.uniform(ks[2], (MLP_DIM, HIDDEN_SIZE // BLOCK_SIZE), dtype=jnp.float32) * 0.1 + 0.001
        up_W_packed = jax.random.randint(ks[3], (MLP_DIM, HIDDEN_SIZE // 2), 0, 32, dtype=jnp.int32)
        up_scales = jax.random.uniform(ks[4], (MLP_DIM, HIDDEN_SIZE // BLOCK_SIZE), dtype=jnp.float32) * 0.1 + 0.001
        down_W_packed = jax.random.randint(ks[5], (HIDDEN_SIZE, MLP_DIM // 2), 0, 32, dtype=jnp.int32)
        down_scales = jax.random.uniform(ks[6], (HIDDEN_SIZE, MLP_DIM // BLOCK_SIZE), dtype=jnp.float32) * 0.1 + 0.001
        return {'x': x, 'gate_W_packed': gate_W_packed, 'gate_scales': gate_scales, 'up_W_packed': up_W_packed, 'up_scales': up_scales, 'down_W_packed': down_W_packed, 'down_scales': down_scales}
    _L0_ffn_all = _L0_ffn_setup()
    _L0_ffn_in = {k: v for k, v in _L0_ffn_all.items() if k in ('gate_W_packed', 'gate_scales', 'up_W_packed', 'up_scales', 'down_W_packed', 'down_scales')}
    del _L0_ffn_all
    return {'x': x, 'ctx_1024': ctx_1024, 'L0_xattn_Wq': _L0_xattn_in['Wq'], 'L0_xattn_Wk': _L0_xattn_in['Wk'], 'L0_xattn_Wv': _L0_xattn_in['Wv'], 'L0_xattn_Wo': _L0_xattn_in['Wo'], 'L0_xattn_gq': _L0_xattn_in['gq'], 'L0_xattn_gk': _L0_xattn_in['gk'], 'L0_ffn_gate_W_packed': _L0_ffn_in['gate_W_packed'], 'L0_ffn_gate_scales': _L0_ffn_in['gate_scales'], 'L0_ffn_up_W_packed': _L0_ffn_in['up_W_packed'], 'L0_ffn_up_scales': _L0_ffn_in['up_scales'], 'L0_ffn_down_W_packed': _L0_ffn_in['down_W_packed'], 'L0_ffn_down_scales': _L0_ffn_in['down_scales']}

def reference(x, ctx_1024, L0_xattn_Wq, L0_xattn_Wk, L0_xattn_Wv, L0_xattn_Wo, L0_xattn_gq, L0_xattn_gk, L0_ffn_gate_W_packed, L0_ffn_gate_scales, L0_ffn_up_W_packed, L0_ffn_up_scales, L0_ffn_down_W_packed, L0_ffn_down_scales):
    import jax
    import jax.numpy as jnp

    def _L0_xattn_ref(hidden_states, encoder_hidden_states, Wq, Wk, Wv, Wo, gq, gk):
        import jax, jax.numpy as jnp
        import numpy as np
        EPS = 1e-05

        def rmsnorm(x, g, eps=EPS):
            var = jnp.mean(jnp.square(x), axis=-1, keepdims=True)
            return x * jax.lax.rsqrt(var + eps) * g
        B, Sq, _ = hidden_states.shape
        Skv = encoder_hidden_states.shape[1]
        D = gq.shape[0]
        H = Wq.shape[1] // D
        scale = 1.0 / np.sqrt(D)
        q = (hidden_states @ Wq).reshape(B, Sq, H, D)
        k = (encoder_hidden_states @ Wk).reshape(B, Skv, H, D)
        v = (encoder_hidden_states @ Wv).reshape(B, Skv, H, D)
        q = rmsnorm(q, gq)
        k = rmsnorm(k, gk)
        scores = jnp.einsum('bqhd,bkhd->bhqk', q, k) * scale
        attn = jax.nn.softmax(scores, axis=-1)
        out = jnp.einsum('bhqk,bkhd->bqhd', attn, v)
        out = out.reshape(B, Sq, H * D)
        return out @ Wo

    def _L0_ffn_ref(x, gate_W_packed, gate_scales, up_W_packed, up_scales, down_W_packed, down_scales):
        import jax, jax.numpy as jnp
        import numpy as np
        BLOCK_SIZE = 32
        HIDDEN_SIZE = 256
        MLP_DIM = 2048
        NVFP4_LUT = jnp.array([0.0, 0.5, 1.0, 1.5, 2.0, 3.0, 4.0, 6.0, 0.0, -0.5, -1.0, -1.5, -2.0, -3.0, -4.0, -6.0], dtype=jnp.float32)

        def dequant_nvfp4(W_packed, scales, block=BLOCK_SIZE):
            N = W_packed.shape[0]
            low = W_packed & 15
            high = W_packed >> 4 & 15
            idx = jnp.stack([low, high], axis=-1).reshape(N, -1)
            vals = NVFP4_LUT[idx]
            K = vals.shape[1]
            vals = vals.reshape(N, K // block, block) * scales[:, :, None]
            return vals.reshape(N, K)
        B, S, H = x.shape
        xt = x.reshape(B * S, H)
        Wg = dequant_nvfp4(gate_W_packed, gate_scales)
        Wu = dequant_nvfp4(up_W_packed, up_scales)
        Wd = dequant_nvfp4(down_W_packed, down_scales)
        gate = jnp.einsum('th,nh->tn', xt, Wg)
        up = jnp.einsum('th,nh->tn', xt, Wu)
        gelu = jnp.tanh(0.7978845608028654 * (gate + 0.044715 * gate ** 3)) * gate * 0.5 + gate * 0.5
        inter = gelu * up
        out = jnp.einsum('tn,hn->th', inter, Wd)
        return out.reshape(B, S, H)
    x = x + _L0_xattn_ref(_layernorm(x, axis=-1), ctx_1024, L0_xattn_Wq, L0_xattn_Wk, L0_xattn_Wv, L0_xattn_Wo, L0_xattn_gq, L0_xattn_gk)
    x = x + _L0_ffn_ref(_layernorm(x, axis=-1), L0_ffn_gate_W_packed, L0_ffn_gate_scales, L0_ffn_up_W_packed, L0_ffn_up_scales, L0_ffn_down_W_packed, L0_ffn_down_scales)
    return x

_drawn_inputs = setup_inputs


def setup_inputs(seed=0):
    import zlib

    import numpy as np

    out = dict(_drawn_inputs(seed))
    spreads = {'L0_xattn_gq': (1.0, 0.2), 'L0_xattn_gk': (1.0, 0.2)}
    factors = {}
    for name, (base, spread) in spreads.items():
        noise = np.random.default_rng([zlib.crc32(name.encode()), seed]).standard_normal(out[name].shape)
        drawn = base * np.exp(spread * noise) if base else spread * noise
        out[name] = jnp.asarray(drawn.astype(out[name].dtype))
    for name, factor in factors.items():
        out[name] = (out[name] * factor).astype(out[name].dtype)
    return out
```

```python
from contextlib import ExitStack

import concourse.bass as bass
from concourse import mybir
from concourse.alu_op_type import AluOpType as ALU

ACT = mybir.ActivationFunctionType
AX_X = mybir.AxisListType.X
F32 = mybir.dt.float32
F16 = mybir.dt.float16
BF16 = mybir.dt.bfloat16
I32 = mybir.dt.int32
U16 = mybir.dt.uint16

P = 128
B, T, DIM = 8, 128, 256
CD = 128
H, D = 16, 128
INNER = H * D
MLP = 2048
BLK = 32
KD = DIM // P
HG = 4
NG = H // HG
NS = B * NG
CH = MLP // (2 * P)
HT = 512
EPS = 1e-5

S_X = 2.0 ** 8
S_W = 2.0 ** 10
S_C = 2.0 ** 7
S_M = 2.0 ** 10
S_Q = 2.0 ** 6
S_K = 2.0 ** 8
S_P = 2.0 ** 10
S_U = 2.0 ** 7
S_F = 2.0 ** 5
S_I = 2.0 ** 3
FP4_BIAS = 2.0 ** 14


def part(view, n, shape):
    names = "abcd"[:len(shape)]
    sizes = dict(zip(names, shape))
    return view[:, 0:n].rearrange(f"p ({' '.join(names)}) -> p {' '.join(names)}", **sizes)


def need(eng, sem, value):
    if not isinstance(value, int) or value > 0:
        eng.wait_ge(sem, value)


def xattn_ffn(nc, x, ctx, ctx_t, wq, wk, wv_t, wo, gq, gk, packed, scales, out):
    with ExitStack() as stack:
        def sb(name, shape, dt):
            return stack.enter_context(nc.sbuf_tensor(name, shape, dt))

        def sem(name):
            return stack.enter_context(nc.semaphore(name))

        bank = [stack.enter_context(nc.psum_tensor(f"bank{i}", [P, 512], F32)) for i in range(8)]

        x_sb = sb("x_sb", [P, B, DIM], F32)
        xt_hi = sb("xt_hi", [P, KD, B * T], F16)
        xt_lo = sb("xt_lo", [P, KD, B * T], F16)
        wq_hi = sb("wq_hi", [P, KD, INNER], F16)
        wq_lo = sb("wq_lo", [P, KD, INNER], F16)
        wk_hi = sb("wk_hi", [P, INNER], F16)
        wk_lo = sb("wk_lo", [P, INNER], F16)
        ct_hi = sb("ct_hi", [P, B * T], F16)
        ct_lo = sb("ct_lo", [P, B * T], F16)
        cx_hi = sb("cx_hi", [P, B * CD], F16)
        cx_lo = sb("cx_lo", [P, B * CD], F16)
        m_hi = sb("m_hi", [P, H, DIM], F16)
        m_lo = sb("m_lo", [P, H, DIM], F16)
        ident = sb("ident", [P, P], F32)
        ones = sb("ones", [P, 1], F32)
        mhalf = sb("mhalf", [P, B], F32)
        gains = sb("gains", [P, 3], F32)

        NF = CH * 3 * DIM
        stage = sb("stage", [P, 2 * NF], F32)
        wq_f = part(stage[:, 0:4096], 4096, (KD, INNER))
        wk_f = stage[:, 4096:6144]
        wv_f = stage[:, 6144:8192]
        wo_f = stage[:, 8192:12288]
        codes = stage[:, 0:NF].bitcast(I32)
        scale_f = stage[:, NF:2 * NF]
        ffn = sb("ffn", [P, 4 * NF], F16)
        wf_hi = ffn[:, 0:2 * NF]
        wf_lo = ffn[:, 2 * NF:4 * NF]
        xn1 = ffn[:, 0:4096].bitcast(F32)
        ct_f = ffn[:, 4096:6144].bitcast(F32)
        cx_f = ffn[:, 6144:8192].bitcast(F32)
        wv_hi, wv_lo = ffn[:, 8192:10240], ffn[:, 10240:12288]
        wo_hi, wo_lo = ffn[:, 12288:16384], ffn[:, 16384:20480]

        q_ring = sb("q_ring", [P, 2, 4, 512], F16)
        k_ring = sb("k_ring", [P, 2, 4, 512], F16)
        u_ring = sb("u_ring", [P, 2, 2, 512], F16)
        pt_ring = sb("pt_ring", [P, 2, 2, 512], F16)
        q_sq = sb("q_sq", [P, 512], F32)
        k_sq = sb("k_sq", [P, HG, T], F32)
        kn = sb("kn", [P, 2, 512], F32)
        prob = sb("prob", [P, 2, 512], F32)
        pn = sb("pn", [P, 2, 512], F32)
        kms = sb("kms", [P, 4, HG], F32)
        kss = sb("kss", [P, 4, HG], F32)
        k_rstd = sb("k_rstd", [P, 4, HG], F32)
        qms = sb("qms", [P, 4, HG], F32)
        q_rstd = sb("q_rstd", [P, 4, HG], F32)
        top = sb("top", [P, 4, HG], F32)
        neg_top = sb("neg_top", [P, 4, HG], F32)
        den = sb("den", [P, 4, HG], F32)
        rden = sb("rden", [P, 4, HG], F32)
        stats = sb("stats", [P, B, 6], F32)
        mean_var = sb("mean_var", [P, B, 2], F32)
        var_eps = sb("var_eps", [P, B], F32)
        rstd = sb("rstd", [P, B], F32)

        def flat(ring):
            return ring[:, :, :, :].rearrange("p a b n -> p (a b n)")
        xn2 = flat(q_ring).bitcast(F32)
        mag = part(flat(k_ring)[:, 0:1536], 1536, (2, 768))
        sgn = part(flat(k_ring)[:, 1536:3072], 1536, (2, 768))
        code16 = flat(k_ring)[:, 3072:3840].bitcast(U16)
        sc_hi = flat(u_ring)[:, 0:768].bitcast(BF16)
        sc_lo = flat(u_ring)[:, 768:1536]
        y = kn[:, :, :].rearrange("p a n -> p (a n)")

        x_in = [sem(f"x_in{i}") for i in range(2)]
        W_NAMES = ("wq0", "wq1", "ct", "wk", "wv", "wo0", "wo1", "cx")
        w_in = {n: sem(f"{n}_in") for n in W_NAMES}
        gains_in, codes_in = sem("gains_in"), sem("codes_in")
        out_done = sem("out_done")
        const_done, gain_done = sem("const_done"), sem("gain_done")
        dve_self = sem("dve_self")
        pool_self = sem("pool_self")
        w_hi, w_lo = sem("w_hi"), sem("w_lo")
        ln_var, ln_rstd, ln_norm = sem("ln_var"), sem("ln_rstd"), sem("ln_norm")
        ln_turned, ln_hi, ln_lo = sem("ln_turned"), sem("ln_hi"), sem("ln_lo")
        m_prod, m_hi_done, m_lo_done = sem("m_prod"), sem("m_hi_done"), sem("m_lo_done")
        k_proj, k_turned, q_proj, q_sumsq = sem("k_proj"), sem("k_turned"), sem("q_proj"), sem("q_sumsq")
        scores, p_turned, mixed, out_proj = sem("scores"), sem("p_turned"), sem("mixed"), sem("out_proj")
        k_squared, kt_hi, q_squared = sem("k_squared"), sem("kt_hi"), sem("q_squared")
        exps, pt_hi = sem("exps"), sem("pt_hi")
        k_summed, k_meansq, k_normed, kt_lo = sem("k_summed"), sem("k_meansq"), sem("k_normed"), sem("kt_lo")
        q_meansq, q_lo, topped, neg_topped = sem("q_meansq"), sem("q_lo"), sem("topped"), sem("neg_topped")
        rden_done, pt_lo, u_hi, u_lo = sem("rden_done"), sem("pt_lo"), sem("u_hi"), sem("u_lo")
        residual = sem("residual")
        k_rstd_done, q_rstd_done, p_normed = sem("k_rstd_done"), sem("q_rstd_done"), sem("p_normed")
        sc_hi_done, decoded = sem("sc_hi_done"), sem("decoded")
        gate_up, gelued, hidden, h_hi, h_lo = (sem(n) for n in ("gate_up", "gelued", "hidden", "h_hi", "h_lo"))
        down, y_done = sem("down"), sem("y_done")

        splits = [
            ("wq0", wq_f[:, 0, :], wq_hi[:, 0, :], wq_lo[:, 0, :], S_W),
            ("wq1", wq_f[:, 1, :], wq_hi[:, 1, :], wq_lo[:, 1, :], S_W),
            ("ct", ct_f, ct_hi[:, :], ct_lo[:, :], S_C),
            ("wk", wk_f, wk_hi[:, :], wk_lo[:, :], S_W),
            ("wv", wv_f, wv_hi, wv_lo, S_W),
            ("wo0", wo_f[:, 0:2048], wo_hi[:, 0:2048], wo_lo[:, 0:2048], S_W),
            ("wo1", wo_f[:, 2048:4096], wo_hi[:, 2048:4096], wo_lo[:, 2048:4096], S_W),
            ("cx", cx_f, cx_hi[:, :], cx_lo[:, :], S_C),
        ]
        MG = H // 2

        def valid(b, off):
            return not isinstance(b, int) or 0 <= NG * b + off < NS

        def steps(eng, step):
            for s in range(-3, NG):
                step(s // NG, s % NG)
            with eng.Fori(1, B - 1) as b:
                for g in range(NG):
                    step(b, g)
            for s in range(NS - NG, NS + 4):
                step(s // NG, s % NG)

        def chunks(eng, chunk):
            chunk(0, 0, True)
            with eng.Fori(1, CH - 1) as c:
                chunk(0, c, True)
            chunk(0, CH - 1, False)
            chunk(1, 0, False)
            with eng.Fori(1, CH) as c:
                chunk(1, c, False)

        block = stack.enter_context(nc.Block())

        @block.sync
        def _(sp):
            x_v = x.rearrange("(b t) n -> t b n", t=T)
            for i in range(2):
                sp.dma_start(x_sb[:, 4 * i:4 * i + 4, :], x_v[:, 4 * i:4 * i + 4, :]).then_inc(x_in[i], 16)
            sp.dma_start(wq_f[:, 0, :], wq[0:P, :]).then_inc(w_in["wq0"], 16)
            sp.dma_start(wq_f[:, 1, :], wq[P:2 * P, :]).then_inc(w_in["wq1"], 16)
            sp.dma_start(ct_f, ctx_t).then_inc(w_in["ct"], 16)
            sp.dma_start(wk_f, wk).then_inc(w_in["wk"], 16)
            sp.dma_start(wv_f, wv_t).then_inc(w_in["wv"], 16)
            wo_v = wo.rearrange("(h d) n -> d h n", d=D)
            for i in range(2):
                sp.dma_start(part(wo_f[:, 2048 * i:2048 * i + 2048], 2048, (8, DIM)),
                             wo_v[:, 8 * i:8 * i + 8, :]).then_inc(w_in[f"wo{i}"], 16)
            sp.dma_start(part(cx_f, 1024, (B, CD)), ctx.rearrange("(b t) c -> t b c", t=T)).then_inc(w_in["cx"], 16)
            sp.wait_ge(w_lo, len(splits))
            sp.dma_start(codes, packed).then_inc(codes_in, 16)
            for i in range(8):
                sp.dma_start(scale_f[16 * i:16 * i + 16, :],
                             scales[i:i + 1, :].broadcast_to([16, NF])).then_inc(codes_in, 16)
            out_v = out.rearrange("(b t) n -> t b n", t=T)
            for half in range(2):
                for i in range(4):
                    sp.wait_ge(y_done, 4 * half + i + 1)
                    sp.dma_start(out_v[:, 4 * half + i, :], y[:, DIM * i:DIM * i + DIM]).then_inc(out_done, 16)
            sp.wait_ge(out_done, 16 * B)

        @block.gpsimd
        def _(pool):
            nc.gpsimd.memset(ident[:, :], 0.0).then_inc(pool_self, 1)
            nc.gpsimd.memset(mhalf[:, :], -0.5).then_inc(pool_self, 1)
            nc.gpsimd.memset(ones[:, :], 1.0).then_inc(pool_self, 1)
            pool.wait_ge(pool_self, 3)
            nc.gpsimd.affine_select(out=ident[:, :], in_=ident[:, :], compare_op=ALU.not_equal, fill=1.0,
                                    base=0, pattern=[[-1, P]], channel_multiplier=1).then_inc(const_done, 1)

            def layer_norm(n):
                pool.wait_ge(ln_var, n)
                nc.gpsimd.tensor_tensor(rstd[:, :], var_eps[:, :], mhalf[:, :], ALU.pow).then_inc(ln_rstd, 1)

            layer_norm(1)

            def step(b, g):
                s = NG * b + g
                if valid(b, g - 1):
                    j, i, q = s - 1, (g - 1) % 2, (g - 1) % 4
                    need(pool, rden_done, j + 1)
                    need(pool, p_turned, j - 1)
                    nc.gpsimd.tensor_tensor(
                        pn[:, i, :].rearrange("p (h k) -> p h k", h=HG),
                        prob[:, i, :].rearrange("p (h k) -> p h k", h=HG),
                        rden[:, q, :].unsqueeze(2).broadcast_to([P, HG, T]), ALU.mult).then_inc(p_normed, 1)
                if valid(b, g + 1):
                    need(pool, q_meansq, s + 2)
                    nc.gpsimd.tensor_tensor(q_rstd[:, (g + 1) % 4, :], qms[:, (g + 1) % 4, :],
                                            mhalf[:, 0:HG], ALU.pow).then_inc(q_rstd_done, 1)
                if valid(b, g + 3):
                    need(pool, k_meansq, s + 4)
                    nc.gpsimd.tensor_tensor(k_rstd[:, (g + 3) % 4, :], kms[:, (g + 3) % 4, :],
                                            mhalf[:, 0:HG], ALU.pow).then_inc(k_rstd_done, 1)

            steps(pool, step)
            layer_norm(2)

        @block.scalar
        def _(act):
            act.dma_start(gains[:, 0:1], gq).then_inc(gains_in, 16)
            act.dma_start(gains[:, 1:2], gk).then_inc(gains_in, 16)

            def split(n):
                name, src, hi, lo, scale = splits[n]
                act.wait_ge(w_in[name], 16)
                nc.scalar.activation(hi, src, ACT.Copy, scale=scale).then_inc(w_hi, 1)

            def layer_norm(n):
                for i in range(4):
                    act.wait_ge(ln_turned, 4 * n + i + 1)
                    nc.scalar.activation(xt_hi[:, :, 256 * i:256 * i + 256],
                                         bank[i][:, :].rearrange("p (k t) -> p k t", k=KD),
                                         ACT.Copy, scale=S_X).then_inc(ln_hi, 1)

            for n in range(4):
                split(n)
            layer_norm(0)
            for n in range(4, len(splits)):
                split(n)
            for i in range(MG):
                act.wait_ge(m_prod, i + 1)
                nc.scalar.activation(m_hi[:, 2 * i:2 * i + 2, :],
                                     bank[4 + i % 4][:, :].rearrange("p (h n) -> p h n", h=2),
                                     ACT.Copy, scale=S_M / S_W ** 2).then_inc(m_hi_done, 1)
            act.wait_ge(gain_done, 1)

            def step(b, g):
                s = NG * b + g
                if valid(b, g - 2):
                    need(act, p_turned, s - 1)
                    nc.scalar.activation(pt_ring[:, 0, (g - 2) % 2, :], bank[2][:, :], ACT.Copy,
                                         scale=S_P).then_inc(pt_hi, 1)
                if valid(b, g):
                    need(act, neg_topped, s + 1)
                    need(act, p_normed, s - 1)
                    for i in range(HG):
                        ins = nc.scalar.activation(prob[:, g % 2, T * i:T * i + T],
                                                   bank[g % 2][:, T * i:T * i + T], ACT.Exp,
                                                   scale=q_rstd[:, g, i:i + 1], bias=neg_top[:, g, i:i + 1],
                                                   accum_out=den[:, g, i:i + 1])
                    ins.then_inc(exps, 1)
                if valid(b, g + 3):
                    need(act, k_proj, s + 4)
                    need(act, k_summed, s + 3)
                    nc.scalar.activation(k_sq[:, :, :].rearrange("p h d -> p (h d)"), bank[4][:, :],
                                         ACT.Square, scale=1.0 / (S_W * S_C)).then_inc(k_squared, 1)
                if valid(b, g + 2):
                    need(act, q_proj, s + 3)
                    nc.scalar.activation(q_ring[:, 0, (g + 2) % 4, :], bank[5][:, :], ACT.Copy,
                                         scale=gains[:, 2:3])
                    nc.scalar.activation(q_sq[:, :], bank[5][:, :], ACT.Square,
                                         scale=1.0 / (S_W * S_X)).then_inc(q_squared, 1)
                    need(act, k_turned, s + 3)
                    nc.scalar.activation(k_ring[:, 0, (g + 2) % 4, :], bank[2][:, :], ACT.Copy,
                                         scale=S_K).then_inc(kt_hi, 1)

            steps(act, step)
            layer_norm(1)

            def scale_hi(c):
                nc.scalar.activation(sc_hi, scale_f[:, bass.ds(c * 768, 768)], ACT.Copy,
                                     scale=S_F * FP4_BIAS).then_inc(sc_hi_done, 1)

            act.wait_ge(codes_in, 16 * 9)
            scale_hi(0)

            def chunk(half, c, decode):
                if decode:
                    need(act, decoded, c + 1)
                    scale_hi(c + 1)
                for i in range(2):
                    u = 2 * (CH * half + c) + i
                    need(act, gate_up, u + 1)
                    need(act, hidden, u - 1)
                    nc.scalar.activation(prob[:, i, :], bank[i][:, :], ACT.Gelu_apprx_tanh,
                                         scale=1.0 / (S_F * S_X)).then_inc(gelued, 1)
                    need(act, hidden, u + 1)
                    need(act, down, u - 1)
                    nc.scalar.activation(pt_ring[:, 0, i, :], pn[:, i, :], ACT.Copy).then_inc(h_hi, 1)

            chunks(act, chunk)

        @block.vector
        def _(dve):
            link_n = [0]

            def link(ins):
                link_n[0] += 1
                ins.then_inc(dve_self, 1)
                dve.wait_ge(dve_self, link_n[0])

            def layer_norm(n, xn):
                for i in range(B):
                    if n == 0 and i % 4 == 0:
                        dve.wait_ge(x_in[i // 4], 16)
                    ins = nc.vector.bn_stats(stats[:, i, :], x_sb[:, i, :])
                link(ins)
                for i in range(B):
                    ins = nc.vector.bn_aggr(mean_var[:, i, :], stats[:, i, :])
                link(ins)
                nc.vector.tensor_scalar(var_eps[:, :], mean_var[:, :, 1], EPS, None, ALU.add).then_inc(ln_var, 1)
                dve.wait_ge(ln_rstd, n + 1)
                for i in range(B):
                    nc.vector.tensor_scalar(xn[:, DIM * i:DIM * i + DIM], x_sb[:, i, :], mean_var[:, i, 0:1],
                                            rstd[:, i:i + 1], ALU.subtract, ALU.mult).then_inc(ln_norm, 1)

            def layer_norm_lo(n):
                for i in range(4):
                    dve.wait_ge(ln_hi, 4 * n + i + 1)
                    nc.vector.scalar_tensor_tensor(
                        out=xt_lo[:, :, 256 * i:256 * i + 256],
                        in0=bank[i][:, :].rearrange("p (k t) -> p k t", k=KD), scalar=S_X,
                        in1=xt_hi[:, :, 256 * i:256 * i + 256],
                        op0=ALU.mult, op1=ALU.subtract).then_inc(ln_lo, 1)

            def split(n):
                name, src, hi, lo, scale = splits[n]
                dve.wait_ge(w_hi, n + 1)
                nc.vector.scalar_tensor_tensor(out=lo, in0=src, scalar=scale, in1=hi, op0=ALU.mult,
                                               op1=ALU.subtract).then_inc(w_lo, 1)

            layer_norm(0, xn1)
            split(0)
            split(1)
            layer_norm_lo(0)
            for n in range(2, len(splits)):
                split(n)
            dve.wait_ge(gains_in, 32)
            nc.vector.scalar_tensor_tensor(out=gains[:, 2:3], in0=gains[:, 0:1], scalar=S_Q / (S_W * S_X),
                                           in1=gains[:, 1:2], op0=ALU.mult, op1=ALU.mult).then_inc(gain_done, 1)
            for i in range(MG):
                dve.wait_ge(m_hi_done, i + 1)
                nc.vector.scalar_tensor_tensor(
                    out=m_lo[:, 2 * i:2 * i + 2, :], in0=bank[4 + i % 4][:, :].rearrange("p (h n) -> p h n", h=2),
                    scalar=S_M / S_W ** 2, in1=m_hi[:, 2 * i:2 * i + 2, :], op0=ALU.mult,
                    op1=ALU.subtract).then_inc(m_lo_done, 1)

            q_c2 = (float(D) ** -0.5 / (S_Q * S_K)) ** 2
            k_c2 = (1.0 / (S_W * S_C)) ** 2

            def step(b, g):
                s = NG * b + g
                if valid(b, g):
                    need(dve, scores, s + 1)
                    nc.vector.reduce_max(top[:, g, :], bank[g % 2][:, :].rearrange("p (h k) -> p h k", h=HG),
                                         AX_X).then_inc(topped, 1)
                if valid(b, g - 1):
                    need(dve, exps, s)
                    nc.vector.reciprocal(rden[:, (g - 1) % 4, :], den[:, (g - 1) % 4, :]).then_inc(rden_done, 1)
                if valid(b, g):
                    need(dve, topped, s + 1)
                    need(dve, q_rstd_done, s + 1)
                    nc.vector.scalar_tensor_tensor(out=neg_top[:, g, :], in0=top[:, g, :], scalar=-1.0,
                                                   in1=q_rstd[:, g, :], op0=ALU.mult,
                                                   op1=ALU.mult).then_inc(neg_topped, 1)
                if valid(b, g - 2):
                    need(dve, pt_hi, s - 1)
                    i = (g - 2) % 2
                    nc.vector.scalar_tensor_tensor(out=pt_ring[:, 1, i, :], in0=bank[2][:, :], scalar=S_P,
                                                   in1=pt_ring[:, 0, i, :], op0=ALU.mult,
                                                   op1=ALU.subtract).then_inc(pt_lo, 1)
                if valid(b, g + 1):
                    need(dve, q_sumsq, s + 2)
                    nc.vector.tensor_scalar(qms[:, (g + 1) % 4, :], bank[7][:, 0:HG], 1.0 / (D * q_c2),
                                            EPS / q_c2, ALU.mult, ALU.add).then_inc(q_meansq, 1)
                if valid(b, g + 2):
                    need(dve, k_rstd_done, s + 3)
                    need(dve, k_turned, s + 1)
                    nc.vector.tensor_tensor(
                        kn[:, g % 2, :].rearrange("p (h d) -> p h d", h=HG),
                        bank[4][:, :].rearrange("p (h d) -> p h d", h=HG),
                        k_rstd[:, (g + 2) % 4, :].unsqueeze(2).broadcast_to([P, HG, D]),
                        ALU.mult).then_inc(k_normed, 1)
                if valid(b, g - 3):
                    i = (g - 3) % 2
                    need(dve, mixed, s - 2)
                    nc.vector.tensor_scalar(u_ring[:, 0, i, :], bank[3][:, :], S_U / (S_C * S_P), None,
                                            ALU.mult).then_inc(u_hi, 1)
                if valid(b, g + 3):
                    need(dve, k_squared, s + 4)
                    nc.vector.reduce_sum(kss[:, (g + 3) % 4, :], k_sq[:, :, :], AX_X).then_inc(k_summed, 1)
                if valid(b, g - 3):
                    need(dve, u_hi, s - 2)
                    nc.vector.scalar_tensor_tensor(out=u_ring[:, 1, i, :], in0=bank[3][:, :],
                                                   scalar=S_U / (S_C * S_P), in1=u_ring[:, 0, i, :],
                                                   op0=ALU.mult, op1=ALU.subtract).then_inc(u_lo, 1)
                if valid(b, g + 3):
                    need(dve, k_summed, s + 4)
                    nc.vector.tensor_scalar(kms[:, (g + 3) % 4, :], kss[:, (g + 3) % 4, :], 1.0 / (D * k_c2),
                                            EPS / k_c2, ALU.mult, ALU.add).then_inc(k_meansq, 1)
                if valid(b, g + 2):
                    i = (g + 2) % 4
                    need(dve, q_squared, s + 3)
                    nc.vector.scalar_tensor_tensor(out=q_ring[:, 1, i, :], in0=bank[5][:, :],
                                                   scalar=gains[:, 2:3], in1=q_ring[:, 0, i, :],
                                                   op0=ALU.mult, op1=ALU.subtract).then_inc(q_lo, 1)
                    need(dve, kt_hi, s + 3)
                    nc.vector.scalar_tensor_tensor(out=k_ring[:, 1, i, :], in0=bank[2][:, :], scalar=S_K,
                                                   in1=k_ring[:, 0, i, :], op0=ALU.mult,
                                                   op1=ALU.subtract).then_inc(kt_lo, 1)
                if g == 3 and valid(b, g - 4):
                    need(dve, out_proj, s - 3)
                    nc.vector.scalar_tensor_tensor(out=x_sb[:, b - 1, :], in0=bank[6][:, 0:DIM],
                                                   scalar=1.0 / (S_M * S_U), in1=x_sb[:, b - 1, :],
                                                   op0=ALU.mult, op1=ALU.add).then_inc(residual, 1)

            steps(dve, step)
            dve.wait_ge(residual, B)
            layer_norm(1, xn2)
            layer_norm_lo(1)

            def decode(c, n):
                def after(k, ins):
                    ins.then_inc(dve_self, 1)
                    dve.wait_ge(dve_self, n + k)
                low = codes[:, bass.ds(c * 768, 768)].bitcast(U16).rearrange("p (n two) -> p n two", two=2)
                after(1, nc.vector.tensor_copy(code16, low[:, :, 0]))
                mag_u, sgn_u = mag.bitcast(U16), sgn.bitcast(U16)
                nc.vector.tensor_scalar(mag_u[:, 0, :], code16, 0x07, 9, ALU.bitwise_and, ALU.logical_shift_left)
                nc.vector.tensor_scalar(sgn_u[:, 0, :], code16, 0x08, 12, ALU.bitwise_and, ALU.logical_shift_left)
                nc.vector.tensor_scalar(mag_u[:, 1, :], code16, 0x70, 5, ALU.bitwise_and, ALU.logical_shift_left)
                after(2, nc.vector.tensor_scalar(sgn_u[:, 1, :], code16, 0x80, 8, ALU.bitwise_and,
                                                 ALU.logical_shift_left))
                nc.vector.tensor_tensor(mag_u, mag_u, sgn_u, ALU.bitwise_or)
                need(dve, sc_hi_done, c + 1)
                after(3, nc.vector.scalar_tensor_tensor(out=sc_lo, in0=scale_f[:, bass.ds(c * 768, 768)],
                                                        scalar=S_F * FP4_BIAS, in1=sc_hi, op0=ALU.mult,
                                                        op1=ALU.subtract))
                for w, sc in ((wf_hi, sc_hi), (wf_lo, sc_lo)):
                    dst = w[:, bass.ds(c * 1536, 1536)].rearrange("p (two n) -> p two n", two=2)
                    ins = nc.vector.tensor_tensor(dst, mag, sc.unsqueeze(1).broadcast_to([P, 2, 768]), ALU.mult)
                ins.then_inc(decoded, 1)

            dve.wait_ge(codes_in, 16 * 9)
            links = link_n[0]
            decode(0, links)

            def chunk(half, c, with_decode):
                for i in range(2):
                    u = 2 * (CH * half + c) + i
                    need(dve, gelued, u + 1)
                    nc.vector.scalar_tensor_tensor(out=pn[:, i, :], in0=bank[2 + i][:, :],
                                                   scalar=S_I / (S_F * S_X), in1=prob[:, i, :],
                                                   op0=ALU.mult, op1=ALU.mult).then_inc(hidden, 1)
                    if i == 0 and with_decode:
                        decode(c + 1, links + 3 * (c + 1))
                    need(dve, h_hi, u + 1)
                    nc.vector.tensor_tensor(pt_ring[:, 1, i, :], pn[:, i, :], pt_ring[:, 0, i, :],
                                            ALU.subtract).then_inc(h_lo, 1)

            def finish(half):
                for i in range(4):
                    dve.wait_ge(down, 2 * CH * (half + 1))
                    if half:
                        dve.wait_ge(out_done, 16 * 4)
                    nc.vector.scalar_tensor_tensor(out=y[:, DIM * i:DIM * i + DIM], in0=bank[4 + i][:, 0:DIM],
                                                   scalar=1.0 / (S_F * S_I), in1=x_sb[:, 4 * half + i, :],
                                                   op0=ALU.mult, op1=ALU.add).then_inc(y_done, 1)

            chunk(0, 0, True)
            with dve.Fori(1, CH - 1) as c:
                chunk(0, c, True)
            chunk(0, CH - 1, False)
            finish(0)
            with dve.Fori(0, CH) as c:
                chunk(1, c, False)
            finish(1)

        @block.tensor
        def _(pe):
            def three(dst, a, b, first=True, last=True):
                (a_hi, a_lo), (b_hi, b_lo) = a, b
                nc.tensor.matmul(dst, a_hi, b_hi, start=first, stop=False)
                nc.tensor.matmul(dst, a_hi, b_lo, start=False, stop=False)
                return nc.tensor.matmul(dst, a_lo, b_hi, start=False, stop=last)

            def layer_norm(n, xn, step):
                for i in range(4):
                    pe.wait_ge(ln_norm, B * n + 2 * i + 2)
                    for k in range(KD):
                        for t in range(2):
                            row = xn[:, DIM * (2 * i + t):DIM * (2 * i + t) + DIM]
                            src = row[:, P * k:P * k + P] if step == 1 else \
                                row.rearrange("p (f two) -> p two f", two=2)[:, k, :]
                            ins = nc.tensor.transpose(bank[i][:, P * (2 * k + t):P * (2 * k + t) + P], src,
                                                      ident[:, :])
                    ins.then_inc(ln_turned, 1)

            pe.wait_ge(const_done, 1)
            layer_norm(0, xn1, 1)
            pe.wait_ge(w_lo, len(splits))
            for i in range(MG):
                if i >= 4:
                    pe.wait_ge(m_lo_done, i - 3)
                for t in range(2):
                    h = 2 * i + t
                    ins = three(bank[4 + i % 4][:, DIM * t:DIM * t + DIM],
                                (wv_hi[:, CD * h:CD * h + CD], wv_lo[:, CD * h:CD * h + CD]),
                                (wo_hi[:, DIM * h:DIM * h + DIM], wo_lo[:, DIM * h:DIM * h + DIM]))
                ins.then_inc(m_prod, 1)
            pe.wait_ge(m_lo_done, MG)
            pe.wait_ge(ln_lo, 4)

            def step(b, g):
                s = NG * b + g
                if valid(b, g):
                    need(pe, q_lo, s + 1)
                    need(pe, kt_lo, s + 1)
                    need(pe, exps, s - 1)
                    for i in range(HG):
                        c = slice(T * i, T * i + T)
                        ins = three(bank[g % 2][:, c], (q_ring[:, 0, g, c], q_ring[:, 1, g, c]),
                                    (k_ring[:, 0, g, c], k_ring[:, 1, g, c]))
                    ins.then_inc(scores, 1)
                if valid(b, g - 2):
                    need(pe, p_normed, s - 1)
                    if valid(b, g + 1):
                        need(pe, kt_lo, s + 2)
                    else:
                        need(pe, pt_lo, s - 2)
                    for i in range(HG):
                        c = slice(T * i, T * i + T)
                        ins = nc.tensor.transpose(bank[2][:, c], pn[:, (g - 2) % 2, c], ident[:, :])
                    ins.then_inc(p_turned, 1)
                if valid(b, g + 1):
                    need(pe, q_squared, s + 2)
                    need(pe, q_meansq, s + 1)
                    for i in range(HG):
                        ins = nc.tensor.matmul(bank[7][:, i:i + 1], q_sq[:, T * i:T * i + T], ones[:, :],
                                               start=True, stop=True)
                    ins.then_inc(q_sumsq, 1)
                if valid(b, g - 3):
                    need(pe, pt_lo, s - 2)
                    need(pe, u_lo, s - 3)
                    bb = b + (g - 3) // NG
                    c = bass.ds(bb * CD, CD)
                    i = (g - 3) % 2
                    three(bank[3][:, :], (cx_hi[:, c], cx_lo[:, c]),
                          (pt_ring[:, 0, i, :], pt_ring[:, 1, i, :])).then_inc(mixed, 1)
                if valid(b, g + 3):
                    need(pe, k_normed, s + 3)
                    bb, gg = b + (g + 3) // NG, (g + 3) % NG
                    c = bass.ds(bb * T, T)
                    w = slice(512 * gg, 512 * gg + 512)
                    three(bank[4][:, :], (ct_hi[:, c], ct_lo[:, c]),
                          (wk_hi[:, w], wk_lo[:, w])).then_inc(k_proj, 1)
                if valid(b, g + 2):
                    need(pe, q_lo, s + 2)
                    bb, gg = b + (g + 2) // NG, (g + 2) % NG
                    c = bass.ds(bb * T, T)
                    for i in range(HG):
                        w = slice(D * (HG * gg + i), D * (HG * gg + i) + D)
                        for k in range(KD):
                            ins = three(bank[5][:, T * i:T * i + T], (wq_hi[:, k, w], wq_lo[:, k, w]),
                                        (xt_hi[:, k, c], xt_lo[:, k, c]), k == 0, k == KD - 1)
                    ins.then_inc(q_proj, 1)
                    need(pe, k_normed, s + 3)
                    if valid(b, g - 2):
                        need(pe, pt_lo, s - 1)
                    else:
                        need(pe, kt_lo, s + 2)
                    for i in range(HG):
                        c = slice(T * i, T * i + T)
                        ins = nc.tensor.transpose(bank[2][:, c], kn[:, g % 2, c], ident[:, :])
                    ins.then_inc(k_turned, 1)
                if valid(b, g - 4):
                    need(pe, u_lo, s - 3)
                    if g == 0:
                        need(pe, residual, b - 1)
                    for i in range(HG):
                        c = slice(T * i, T * i + T)
                        ins = three(bank[6][:, 0:DIM], (u_ring[:, 0, g % 2, c], u_ring[:, 1, g % 2, c]),
                                    (m_hi[:, HG * g + i, :], m_lo[:, HG * g + i, :]),
                                    g == 0 and i == 0, g == NG - 1 and i == HG - 1)
                    ins.then_inc(out_proj, 1)

            steps(pe, step)
            layer_norm(1, xn2, 2)
            pe.wait_ge(ln_lo, 8)

            def gate_up_proj(half, c, i):
                u = 2 * (CH * half + c) + i
                need(pe, hidden, u - 1)
                for mat in range(2):
                    for k in range(KD):
                        w = bass.ds(c * 1536 + (768 * k + 256 * mat + P * i), P)
                        t = slice(HT * half, HT * half + HT)
                        ins = three(bank[2 * mat + i][:, :], (wf_hi[:, w], wf_lo[:, w]),
                                    (xt_hi[:, k, t], xt_lo[:, k, t]), k == 0, k == KD - 1)
                ins.then_inc(gate_up, 1)

            def down_proj(half, c, i, first=False, last=False):
                u = 2 * (CH * half + c) + i
                need(pe, h_lo, u + 1)
                w = bass.ds(c * 1536 + (768 * i + 512), DIM)
                for t in range(4):
                    a = slice(P * t, P * t + P)
                    ins = three(bank[4 + t][:, 0:DIM], (pt_ring[:, 0, i, a], pt_ring[:, 1, i, a]),
                                (wf_hi[:, w], wf_lo[:, w]), first, last)
                ins.then_inc(down, 1)

            for half in range(2):
                if half:
                    pe.wait_ge(y_done, 4)
                need(pe, decoded, 1)
                gate_up_proj(half, 0, 0)
                gate_up_proj(half, 0, 1)
                down_proj(half, 0, 0, first=True)
                with pe.Fori(1, CH) as c:
                    if half == 0:
                        need(pe, decoded, c + 1)
                    gate_up_proj(half, c, 0)
                    down_proj(half, c - 1, 1)
                    gate_up_proj(half, c, 1)
                    down_proj(half, c, 0)
                down_proj(half, CH - 1, 1, last=True)


def kernel(**inputs):
    import numpy as np
    import concourse.bacc as bacc
    from concourse.bass_utils import run_bass_kernel_spmd

    a = {n: np.asarray(v) for n, v in inputs.items()}

    def columns(w):
        return w.T.reshape(w.shape[1], CH, P, 2).transpose(0, 1, 3, 2).reshape(w.shape[1], CH, 2 * P)

    dp, ds = a["L0_ffn_down_W_packed"], a["L0_ffn_down_scales"]
    down_codes = dp.T.reshape(CH, P, DIM).transpose(1, 0, 2)
    down_scales = ds.T.reshape(CH, 2 * P // BLK, DIM).transpose(1, 0, 2)
    codes = np.stack([columns(a["L0_ffn_gate_W_packed"]), columns(a["L0_ffn_up_W_packed"]), down_codes], axis=2)
    scales = np.stack([columns(a["L0_ffn_gate_scales"]), columns(a["L0_ffn_up_scales"]), down_scales], axis=2)
    arrays = {
        "x": a["x"].reshape(B * T, DIM),
        "ctx": a["ctx_1024"].reshape(B * T, CD),
        "ctx_t": a["ctx_1024"].reshape(B * T, CD).T,
        "wq": a["L0_xattn_Wq"],
        "wk": a["L0_xattn_Wk"],
        "wv_t": a["L0_xattn_Wv"].reshape(CD, H, D).transpose(2, 1, 0).reshape(D, H * CD),
        "wo": a["L0_xattn_Wo"],
        "gq": a["L0_xattn_gq"].reshape(D, 1),
        "gk": a["L0_xattn_gk"].reshape(D, 1),
        "packed": codes.reshape(P, CH * 3 * DIM),
        "scales": scales.reshape(8, CH * 3 * DIM),
    }
    arrays = {n: np.ascontiguousarray(v) for n, v in arrays.items()}
    nc = bacc.Bacc("TRN2", target_bir_lowering=False, num_devices=1)
    args = [nc.dram_tensor(n, v.shape, mybir.dt.from_np(v.dtype), kind="ExternalInput").ap()
            for n, v in arrays.items()]
    out = nc.dram_tensor("out", (B * T, DIM), F32, kind="ExternalOutput").ap()
    xattn_ffn(nc, *args, out)
    r = run_bass_kernel_spmd(nc, [arrays], core_ids=[0])
    return r.results[0]["out"].reshape(B, T, DIM)
```

```python
from contextlib import ExitStack

import concourse.bass as bass
from concourse import mybir
from concourse.alu_op_type import AluOpType as ALU

ACT = mybir.ActivationFunctionType
AX_X = mybir.AxisListType.X
F32 = mybir.dt.float32
F16 = mybir.dt.float16
BF16 = mybir.dt.bfloat16
I32 = mybir.dt.int32
U16 = mybir.dt.uint16

P = 128
B, T, DIM = 8, 128, 256
CD = 128
H, D = 16, 128
INNER = H * D
MLP = 2048
BLK = 32
KD = DIM // P
HG = 4
NG = H // HG
NS = B * NG
CH = MLP // (2 * P)
HT = 512
EPS = 1e-5

S_X = 2.0 ** 8
S_W = 2.0 ** 10
S_C = 2.0 ** 7
S_M = 2.0 ** 10
S_Q = 2.0 ** 6
S_K = 2.0 ** 8
S_P = 2.0 ** 10
S_U = 2.0 ** 7
S_F = 2.0 ** 5
S_I = 2.0 ** 3
FP4_BIAS = 2.0 ** 14


def part(view, n, shape):
    names = "abcd"[:len(shape)]
    sizes = dict(zip(names, shape))
    return view[:, 0:n].rearrange(f"p ({' '.join(names)}) -> p {' '.join(names)}", **sizes)


def need(eng, sem, value):
    if not isinstance(value, int) or value > 0:
        eng.wait_ge(sem, value)


def xattn_ffn(nc, x, ctx, ctx_t, wq, wk, wv_t, wo, gq, gk, packed, scales, out):
    with ExitStack() as stack:
        def sb(name, shape, dt):
            return stack.enter_context(nc.sbuf_tensor(name, shape, dt))

        def sem(name):
            return stack.enter_context(nc.semaphore(name))

        bank = [stack.enter_context(nc.psum_tensor(f"bank{i}", [P, 512], F32)) for i in range(8)]

        x_sb = sb("x_sb", [P, B, DIM], F32)
        xt_hi = sb("xt_hi", [P, KD, B * T], F16)
        xt_lo = sb("xt_lo", [P, KD, B * T], F16)
        wq_hi = sb("wq_hi", [P, KD, INNER], F16)
        wq_lo = sb("wq_lo", [P, KD, INNER], F16)
        wk_hi = sb("wk_hi", [P, INNER], F16)
        wk_lo = sb("wk_lo", [P, INNER], F16)
        ct_hi = sb("ct_hi", [P, B * T], F16)
        ct_lo = sb("ct_lo", [P, B * T], F16)
        cx_hi = sb("cx_hi", [P, B * CD], F16)
        cx_lo = sb("cx_lo", [P, B * CD], F16)
        m_hi = sb("m_hi", [P, H, DIM], F16)
        m_lo = sb("m_lo", [P, H, DIM], F16)
        ident = sb("ident", [P, P], F32)
        ones = sb("ones", [P, 1], F32)
        mhalf = sb("mhalf", [P, B], F32)
        gains = sb("gains", [P, 3], F32)

        NF = CH * 3 * DIM
        stage = sb("stage", [P, 2 * NF], F32)
        wq_f = part(stage[:, 0:4096], 4096, (KD, INNER))
        wk_f = stage[:, 4096:6144]
        wv_f = stage[:, 6144:8192]
        wo_f = stage[:, 8192:12288]
        codes = stage[:, 0:NF].bitcast(I32)
        scale_f = stage[:, NF:2 * NF]
        ffn = sb("ffn", [P, 4 * NF], F16)
        wf_hi = ffn[:, 0:2 * NF]
        wf_lo = ffn[:, 2 * NF:4 * NF]
        xn1 = ffn[:, 0:4096].bitcast(F32)
        ct_f = ffn[:, 4096:6144].bitcast(F32)
        cx_f = ffn[:, 6144:8192].bitcast(F32)
        wv_hi, wv_lo = ffn[:, 8192:10240], ffn[:, 10240:12288]
        wo_hi, wo_lo = ffn[:, 12288:16384], ffn[:, 16384:20480]

        q_ring = sb("q_ring", [P, 2, 2, 512], F16)
        k_ring = sb("k_ring", [P, 2, 2, 512], F16)
        u_ring = sb("u_ring", [P, 2, 2, 512], F16)
        pt_ring = sb("pt_ring", [P, 2, 2, 512], F16)
        q_sq = sb("q_sq", [P, 512], F32)
        k_sq = sb("k_sq", [P, HG, T], F32)
        kn = sb("kn", [P, 2, 512], F32)
        prob = sb("prob", [P, 2, 512], F32)
        pn = sb("pn", [P, 2, 512], F32)
        kms = sb("kms", [P, 4, HG], F32)
        kss = sb("kss", [P, 4, HG], F32)
        k_rstd = sb("k_rstd", [P, 4, HG], F32)
        qms = sb("qms", [P, 4, HG], F32)
        q_rstd = sb("q_rstd", [P, 4, HG], F32)
        top = sb("top", [P, 4, HG], F32)
        neg_top = sb("neg_top", [P, 4, HG], F32)
        den = sb("den", [P, 4, HG], F32)
        rden = sb("rden", [P, 4, HG], F32)
        stats = sb("stats", [P, B, 6], F32)
        mean_var = sb("mean_var", [P, B, 2], F32)
        var_eps = sb("var_eps", [P, B], F32)
        rstd = sb("rstd", [P, B], F32)
        ln2_raw = sb("ln2_raw", [P, 6], F32)
        ln2_small = sb("ln2_small", [P, 4], F32)
        xn2 = sb("xn2", [P, DIM], F32)

        CW = 3 * DIM
        code16 = sb("code16", [P, CW], U16)
        sign16 = sb("sign16", [P, CW], U16)
        sc_hi = sb("sc_hi", [P, CW], BF16)
        sc_lo = sb("sc_lo", [P, CW], F16)
        y = kn[:, :, :].rearrange("p a n -> p (a n)")

        def code_chunk(c):
            return codes[:, bass.ds(c * CW, CW)].bitcast(U16)

        x_in = [sem(f"x_in{i}") for i in range(2)]
        W_NAMES = ("ct", "wk", "wq0", "wq1", "wv", "wo0", "cx", "wo1")
        w_in = {n: sem(f"{n}_in") for n in W_NAMES}
        gains_in, codes_in = sem("gains_in"), sem("codes_in")
        out_done = sem("out_done")
        const_done, gain_done = sem("const_done"), sem("gain_done")
        dve_self = sem("dve_self")
        pool_self = sem("pool_self")
        w_hi, w_lo = sem("w_hi"), sem("w_lo")
        v_scaled, v_hi, v_lo = sem("v_scaled"), sem("v_hi"), sem("v_lo")
        ln_var, ln_rstd, ln_norm = sem("ln_var"), sem("ln_rstd"), sem("ln_norm")
        ln_turned, ln_hi, ln_lo = sem("ln_turned"), sem("ln_hi"), sem("ln_lo")
        m_prod, m_hi_done, m_lo_done = sem("m_prod"), sem("m_hi_done"), sem("m_lo_done")
        k_proj, k_turned, q_proj, q_sumsq = sem("k_proj"), sem("k_turned"), sem("q_proj"), sem("q_sumsq")
        scores, p_turned, mixed, out_proj = sem("scores"), sem("p_turned"), sem("mixed"), sem("out_proj")
        k_squared, kt_hi, q_squared = sem("k_squared"), sem("kt_hi"), sem("q_squared")
        exps, pt_hi = sem("exps"), sem("pt_hi")
        k_summed, k_meansq, k_normed, kt_lo = sem("k_summed"), sem("k_meansq"), sem("k_normed"), sem("kt_lo")
        q_meansq, q_lo, topped, neg_topped = sem("q_meansq"), sem("q_lo"), sem("topped"), sem("neg_topped")
        rden_done, pt_lo, u_hi, u_lo = sem("rden_done"), sem("pt_lo"), sem("u_hi"), sem("u_lo")
        residual = sem("residual")
        k_rstd_done, q_rstd_done, p_normed = sem("k_rstd_done"), sem("q_rstd_done"), sem("p_normed")
        coded, signed, joined = sem("coded"), sem("signed"), sem("joined")
        sc_hi_done, sc_lo_done = sem("sc_hi_done"), sem("sc_lo_done")
        hi_decoded, decoded = sem("hi_decoded"), sem("decoded")
        ln2_stats, ln2_mean, ln2_var, ln2_rstd = (sem(f"ln2_{n}") for n in ("stats", "mean", "var", "rstd"))
        ln2_norm, ln2_turned, ln2_hi, ln2_lo = (sem(f"ln2_{n}") for n in ("norm", "turned", "hi", "lo"))
        gate_up, gelued, hidden, h_hi, h_lo = (sem(n) for n in ("gate_up", "gelued", "hidden", "h_hi", "h_lo"))
        down, y_done = sem("down"), sem("y_done")

        splits = [
            ("ct", ct_f, ct_hi[:, :], ct_lo[:, :], S_C),
            ("wk", wk_f, wk_hi[:, :], wk_lo[:, :], S_W),
            ("wq0", wq_f[:, 0, :], wq_hi[:, 0, :], wq_lo[:, 0, :], S_W),
            ("wq1", wq_f[:, 1, :], wq_hi[:, 1, :], wq_lo[:, 1, :], S_W),
            ("cx", cx_f, cx_hi[:, :], cx_lo[:, :], S_C),
        ]
        pool_splits = [
            ("wv", wv_f, wv_hi, wv_lo),
            ("wo0", wo_f[:, 0:2048], wo_hi[:, 0:2048], wo_lo[:, 0:2048]),
            ("wo1", wo_f[:, 2048:4096], wo_hi[:, 2048:4096], wo_lo[:, 2048:4096]),
        ]
        MG = H // 2

        def valid(b, off):
            return not isinstance(b, int) or 0 <= NG * b + off < NS

        def ln_valid(b):
            return not isinstance(b, int) or 2 <= b < B + 2

        def code_valid(b):
            return not isinstance(b, int) or 1 <= b < B + 1

        def steps(eng, step, between=None):
            for s in range(-3, 2 * NG):
                step(s // NG, s % NG)
                if between and s in between:
                    between[s]()
            with eng.Fori(2, B - 1) as b:
                for g in range(NG):
                    step(b, g)
            for s in range(NS - NG, NS + 4):
                step(s // NG, s % NG)

        LN_PARTS = [(0, 2), (2, B)]
        LN_BANK = [0, 3, 6, 3]
        M_BANK = [6, 3, 6, 3, 6, 3, 6, 3]

        block = stack.enter_context(nc.Block())

        @block.sync
        def _(sp):
            x_v = x.rearrange("(b t) n -> t b n", t=T)
            wo_v = wo.rearrange("(h d) n -> d h n", d=D)

            def load_wo(i):
                sp.dma_start(part(wo_f[:, 2048 * i:2048 * i + 2048], 2048, (8, DIM)),
                             wo_v[:, 8 * i:8 * i + 8, :]).then_inc(w_in[f"wo{i}"], 16)

            sp.dma_start(x_sb[:, 0:2, :], x_v[:, 0:2, :]).then_inc(x_in[0], 16)
            sp.dma_start(ct_f, ctx_t).then_inc(w_in["ct"], 16)
            sp.dma_start(wk_f, wk).then_inc(w_in["wk"], 16)
            sp.dma_start(wq_f[:, 0, :], wq[0:P, :]).then_inc(w_in["wq0"], 16)
            sp.dma_start(wq_f[:, 1, :], wq[P:2 * P, :]).then_inc(w_in["wq1"], 16)
            sp.dma_start(x_sb[:, 2:B, :], x_v[:, 2:B, :]).then_inc(x_in[1], 16)
            sp.dma_start(wv_f, wv_t).then_inc(w_in["wv"], 16)
            load_wo(0)
            sp.dma_start(part(cx_f, 1024, (B, CD)), ctx.rearrange("(b t) c -> t b c", t=T)).then_inc(w_in["cx"], 16)
            load_wo(1)
            sp.wait_ge(w_lo, 4)
            sp.wait_ge(v_lo, len(pool_splits))
            sp.dma_start(codes, packed).then_inc(codes_in, 16)
            for i in range(8):
                sp.dma_start(scale_f[16 * i:16 * i + 16, :],
                             scales[i:i + 1, :].broadcast_to([16, NF])).then_inc(codes_in, 16)
            out_v = out.rearrange("(b t) n -> t b n", t=T)
            for half in range(2):
                for i in range(4):
                    sp.wait_ge(y_done, 4 * half + i + 1)
                    sp.dma_start(out_v[:, 4 * half + i, :], y[:, DIM * i:DIM * i + DIM]).then_inc(out_done, 16)
            sp.wait_ge(out_done, 16 * B)

        @block.gpsimd
        def _(pool):
            nc.gpsimd.memset(ident[:, :], 0.0).then_inc(pool_self, 1)
            nc.gpsimd.memset(mhalf[:, :], -0.5).then_inc(pool_self, 1)
            nc.gpsimd.memset(ones[:, :], 1.0).then_inc(pool_self, 1)
            pool.wait_ge(pool_self, 3)
            nc.gpsimd.affine_select(out=ident[:, :], in_=ident[:, :], compare_op=ALU.not_equal, fill=1.0,
                                    base=0, pattern=[[-1, P]], channel_multiplier=1).then_inc(const_done, 1)

            def ln_root(n):
                pool.wait_ge(ln_var, n + 1)
                a, b = LN_PARTS[n]
                nc.gpsimd.tensor_tensor(rstd[:, a:b], var_eps[:, a:b], mhalf[:, a:b], ALU.pow).then_inc(ln_rstd, 1)

            def scale(n):
                name, src, _, _ = pool_splits[n]
                pool.wait_ge(w_in[name], 16)
                nc.gpsimd.tensor_scalar(src, src, S_W, 1.0, ALU.mult, ALU.mult).then_inc(v_scaled, 1)

            def low(n):
                _, src, hi, lo = pool_splits[n]
                pool.wait_ge(v_hi, n + 1)
                nc.gpsimd.tensor_tensor(lo, src, hi, ALU.subtract).then_inc(v_lo, 1)

            def weights(b, n):
                c = b - 2
                w, sc = ((wf_hi, sc_hi), (wf_lo, sc_lo))[n // 3]
                if n == 0:
                    need(pool, codes_in, 16 * 9)
                    need(pool, joined, 2 * c + 2)
                    need(pool, sc_hi_done, c + 1)
                if n == 3:
                    need(pool, sc_lo_done, c + 1)
                k = slice(DIM * (n % 3), DIM * (n % 3) + DIM)
                mags = code_chunk(c).bitcast(F16).rearrange("p (two n) -> p two n", two=2)
                dst = w[:, bass.ds(c * 2 * CW, 2 * CW)].rearrange("p (two n) -> p two n", two=2)
                ins = nc.gpsimd.tensor_tensor(dst[:, :, k], mags[:, :, k],
                                              sc[:, k].unsqueeze(1).broadcast_to([P, 2, DIM]), ALU.mult)
                if n == 2:
                    ins.then_inc(hi_decoded, 1)
                if n == 5:
                    ins.then_inc(decoded, 1)

            PIECES = ((0, 1), (2,), (3, 4), (5,))

            ln_root(0)
            scale(0)
            scale(1)

            def step(b, g):
                s = NG * b + g
                if valid(b, g - 1):
                    j, i, q = s - 1, (g - 1) % 2, (g - 1) % 4
                    need(pool, rden_done, j + 1)
                    need(pool, p_turned, j - 1)
                    nc.gpsimd.tensor_tensor(
                        pn[:, i, :].rearrange("p (h k) -> p h k", h=HG),
                        prob[:, i, :].rearrange("p (h k) -> p h k", h=HG),
                        rden[:, q, :].unsqueeze(2).broadcast_to([P, HG, T]), ALU.mult).then_inc(p_normed, 1)
                if valid(b, g + 1):
                    need(pool, q_meansq, s + 2)
                    nc.gpsimd.tensor_tensor(q_rstd[:, (g + 1) % 4, :], qms[:, (g + 1) % 4, :],
                                            mhalf[:, 0:HG], ALU.pow).then_inc(q_rstd_done, 1)
                if valid(b, g + 3):
                    need(pool, k_meansq, s + 4)
                    nc.gpsimd.tensor_tensor(k_rstd[:, (g + 3) % 4, :], kms[:, (g + 3) % 4, :],
                                            mhalf[:, 0:HG], ALU.pow).then_inc(k_rstd_done, 1)
                if g == 1 and ln_valid(b):
                    need(pool, ln2_var, b - 1)
                    nc.gpsimd.tensor_tensor(ln2_small[:, 3:4], ln2_small[:, 2:3], mhalf[:, 0:1],
                                            ALU.pow).then_inc(ln2_rstd, 1)
                if ln_valid(b):
                    for n in PIECES[g]:
                        weights(b, n)

            steps(pool, step, {-3: lambda: scale(2), -2: lambda: (ln_root(1), low(0)), -1: lambda: low(1),
                               0: lambda: low(2)})
            for g in range(NG):
                step(B + 1, g)

        @block.scalar
        def _(act):
            act.dma_start(gains[:, 0:1], gq).then_inc(gains_in, 16)
            act.dma_start(gains[:, 1:2], gk).then_inc(gains_in, 16)

            def split(n):
                name, src, hi, lo, scale = splits[n]
                act.wait_ge(w_in[name], 16)
                nc.scalar.activation(hi, src, ACT.Copy, scale=scale).then_inc(w_hi, 1)

            def pool_split(n):
                act.wait_ge(v_scaled, n + 1)
                nc.scalar.activation(pool_splits[n][2], pool_splits[n][1], ACT.Copy).then_inc(v_hi, 1)

            def ln_high(i):
                act.wait_ge(ln_turned, i + 1)
                nc.scalar.activation(xt_hi[:, :, 256 * i:256 * i + 256],
                                     bank[LN_BANK[i]][:, :].rearrange("p (k t) -> p k t", k=KD),
                                     ACT.Copy, scale=S_X).then_inc(ln_hi, 1)

            def m_high(i):
                act.wait_ge(m_prod, i + 1)
                nc.scalar.activation(m_hi[:, 2 * i:2 * i + 2, :],
                                     bank[M_BANK[i]][:, :].rearrange("p (h n) -> p h n", h=2),
                                     ACT.Copy, scale=S_M / S_W ** 2).then_inc(m_hi_done, 1)

            split(0)
            split(1)
            split(2)
            ln_high(0)
            split(3)
            act.wait_ge(gain_done, 1)

            def step(b, g):
                s = NG * b + g
                if valid(b, g - 2):
                    need(act, p_turned, s - 1)
                    nc.scalar.activation(pt_ring[:, 0, (g - 2) % 2, :], bank[2][:, :], ACT.Copy,
                                         scale=S_P).then_inc(pt_hi, 1)
                if g == 3 and ln_valid(b):
                    need(act, ln2_turned, b - 1)
                    nc.scalar.activation(xt_hi[:, :, bass.ds((b - 2) * T, T)],
                                         bank[7][:, 256:512].rearrange("p (k t) -> p k t", k=KD),
                                         ACT.Copy, scale=S_X).then_inc(ln2_hi, 1)
                if valid(b, g):
                    need(act, neg_topped, s + 1)
                    need(act, p_normed, s - 1)
                    for i in range(HG):
                        ins = nc.scalar.activation(prob[:, g % 2, T * i:T * i + T],
                                                   bank[g % 2][:, T * i:T * i + T], ACT.Exp,
                                                   scale=q_rstd[:, g, i:i + 1], bias=neg_top[:, g, i:i + 1],
                                                   accum_out=den[:, g, i:i + 1])
                    ins.then_inc(exps, 1)
                if valid(b, g - 3):
                    need(act, mixed, s - 2)
                    nc.scalar.activation(u_ring[:, 0, (g - 3) % 2, :], bank[3][:, :], ACT.Copy,
                                         scale=S_U / (S_C * S_P)).then_inc(u_hi, 1)
                if valid(b, g + 2):
                    need(act, k_turned, s + 3)
                    nc.scalar.activation(k_ring[:, 0, g % 2, :], bank[2][:, :], ACT.Copy,
                                         scale=S_K).then_inc(kt_hi, 1)
                if valid(b, g + 3):
                    need(act, k_proj, s + 4)
                    need(act, k_summed, s + 3)
                    nc.scalar.activation(k_sq[:, :, :].rearrange("p h d -> p (h d)"), bank[4][:, :],
                                         ACT.Square, scale=1.0 / (S_W * S_C)).then_inc(k_squared, 1)
                if valid(b, g + 2):
                    need(act, q_proj, s + 3)
                    nc.scalar.activation(q_ring[:, 0, g % 2, :], bank[5][:, :], ACT.Copy,
                                         scale=gains[:, 2:3])
                    nc.scalar.activation(q_sq[:, :], bank[5][:, :], ACT.Square,
                                         scale=1.0 / (S_W * S_X)).then_inc(q_squared, 1)
                if g == 3 and code_valid(b):
                    if isinstance(b, int) and b == 1:
                        act.wait_ge(codes_in, 16 * 9)
                    need(act, hi_decoded, b - 1)
                    nc.scalar.activation(sc_hi[:, :], scale_f[:, bass.ds((b - 1) * CW, CW)], ACT.Copy,
                                         scale=S_F * FP4_BIAS).then_inc(sc_hi_done, 1)

            steps(act, step, {-3: lambda: pool_split(0), -2: lambda: pool_split(1),
                              -1: lambda: (ln_high(1), split(4)),
                              0: lambda: (ln_high(2), ln_high(3), pool_split(2)),
                              1: lambda: [m_high(i) for i in range(4)],
                              2: lambda: [m_high(i) for i in range(4, MG)]})
            step(B + 1, 3)

            def chunk(half, c):
                for i in range(2):
                    u = 2 * (CH * half + c) + i
                    need(act, gate_up, u + 1)
                    need(act, hidden, u - 1)
                    nc.scalar.activation(prob[:, i, :], bank[i][:, :], ACT.Gelu_apprx_tanh,
                                         scale=1.0 / (S_F * S_X)).then_inc(gelued, 1)
                    need(act, hidden, u + 1)
                    need(act, down, u - 1)
                    nc.scalar.activation(pt_ring[:, 0, i, :], pn[:, i, :], ACT.Copy).then_inc(h_hi, 1)

            for half in range(2):
                chunk(half, 0)
                with act.Fori(1, CH) as c:
                    chunk(half, c)

        @block.vector
        def _(dve):
            link_n = [0]

            def link(ins):
                link_n[0] += 1
                ins.then_inc(dve_self, 1)
                dve.wait_ge(dve_self, link_n[0])

            def ln_stats(n):
                a, b = LN_PARTS[n]
                dve.wait_ge(x_in[n], 16)
                for i in range(a, b):
                    ins = nc.vector.bn_stats(stats[:, i, :], x_sb[:, i, :])
                link(ins)
                for i in range(a, b):
                    ins = nc.vector.bn_aggr(mean_var[:, i, :], stats[:, i, :])
                link(ins)
                nc.vector.tensor_scalar(var_eps[:, a:b], mean_var[:, a:b, 1], EPS, None, ALU.add).then_inc(ln_var, 1)

            def ln_norms(n):
                dve.wait_ge(ln_rstd, n + 1)
                for i in range(*LN_PARTS[n]):
                    nc.vector.tensor_scalar(xn1[:, DIM * i:DIM * i + DIM], x_sb[:, i, :], mean_var[:, i, 0:1],
                                            rstd[:, i:i + 1], ALU.subtract, ALU.mult).then_inc(ln_norm, 1)

            def ln_low(i):
                dve.wait_ge(ln_hi, i + 1)
                nc.vector.scalar_tensor_tensor(
                    out=xt_lo[:, :, 256 * i:256 * i + 256],
                    in0=bank[LN_BANK[i]][:, :].rearrange("p (k t) -> p k t", k=KD), scalar=S_X,
                    in1=xt_hi[:, :, 256 * i:256 * i + 256], op0=ALU.mult, op1=ALU.subtract).then_inc(ln_lo, 1)

            def split(n):
                name, src, hi, lo, scale = splits[n]
                dve.wait_ge(w_hi, n + 1)
                nc.vector.scalar_tensor_tensor(out=lo, in0=src, scalar=scale, in1=hi, op0=ALU.mult,
                                               op1=ALU.subtract).then_inc(w_lo, 1)

            def m_low(i):
                dve.wait_ge(m_hi_done, i + 1)
                nc.vector.scalar_tensor_tensor(
                    out=m_lo[:, 2 * i:2 * i + 2, :], in0=bank[M_BANK[i]][:, :].rearrange("p (h n) -> p h n", h=2),
                    scalar=S_M / S_W ** 2, in1=m_hi[:, 2 * i:2 * i + 2, :], op0=ALU.mult,
                    op1=ALU.subtract).then_inc(m_lo_done, 1)

            dve.wait_ge(gains_in, 32)
            nc.vector.scalar_tensor_tensor(out=gains[:, 2:3], in0=gains[:, 0:1], scalar=S_Q / (S_W * S_X),
                                           in1=gains[:, 1:2], op0=ALU.mult, op1=ALU.mult).then_inc(gain_done, 1)
            ln_stats(0)
            split(0)
            ln_norms(0)
            split(1)
            split(2)
            ln_low(0)
            split(3)

            q_c2 = (float(D) ** -0.5 / (S_Q * S_K)) ** 2
            k_c2 = (1.0 / (S_W * S_C)) ** 2

            def signs(b, n):
                need(dve, joined, 2 * b + n)
                mask, up = ((0x08, 12), (0x80, 8))[n]
                nc.vector.tensor_scalar(sign16[:, :], code16[:, :], mask, up, ALU.bitwise_and,
                                        ALU.logical_shift_left)

            def magnitude(b, n):
                mask, up = ((0x07, 9), (0x70, 5))[n]
                nc.vector.tensor_scalar(code_chunk(b)[:, CW * n:CW * n + CW], code16[:, :], mask, up,
                                        ALU.bitwise_and, ALU.logical_shift_left).then_inc(signed, 1)

            def join(b, n):
                need(dve, signed, 2 * b + n + 1)
                dst = code_chunk(b)[:, CW * n:CW * n + CW]
                nc.vector.tensor_tensor(dst, dst, sign16[:, :], ALU.bitwise_or).then_inc(joined, 1)

            def step(b, g):
                s = NG * b + g
                if valid(b, g):
                    need(dve, scores, s + 1)
                    nc.vector.reduce_max(top[:, g, :], bank[g % 2][:, :].rearrange("p (h k) -> p h k", h=HG),
                                         AX_X).then_inc(topped, 1)
                if valid(b, g - 1):
                    need(dve, exps, s)
                    nc.vector.reciprocal(rden[:, (g - 1) % 4, :], den[:, (g - 1) % 4, :]).then_inc(rden_done, 1)
                if valid(b, g):
                    need(dve, topped, s + 1)
                    need(dve, q_rstd_done, s + 1)
                    nc.vector.scalar_tensor_tensor(out=neg_top[:, g, :], in0=top[:, g, :], scalar=-1.0,
                                                   in1=q_rstd[:, g, :], op0=ALU.mult,
                                                   op1=ALU.mult).then_inc(neg_topped, 1)
                if valid(b, g + 2):
                    need(dve, k_rstd_done, s + 3)
                    need(dve, k_turned, s + 1)
                    nc.vector.tensor_tensor(
                        kn[:, g % 2, :].rearrange("p (h d) -> p h d", h=HG),
                        bank[4][:, :].rearrange("p (h d) -> p h d", h=HG),
                        k_rstd[:, (g + 2) % 4, :].unsqueeze(2).broadcast_to([P, HG, D]),
                        ALU.mult).then_inc(k_normed, 1)
                if valid(b, g - 2):
                    need(dve, pt_hi, s - 1)
                    i = (g - 2) % 2
                    nc.vector.scalar_tensor_tensor(out=pt_ring[:, 1, i, :], in0=bank[2][:, :], scalar=S_P,
                                                   in1=pt_ring[:, 0, i, :], op0=ALU.mult,
                                                   op1=ALU.subtract).then_inc(pt_lo, 1)
                if g == 3 and ln_valid(b):
                    need(dve, ln2_hi, b - 1)
                    cols = bass.ds((b - 2) * T, T)
                    nc.vector.scalar_tensor_tensor(
                        out=xt_lo[:, :, cols], in0=bank[7][:, 256:512].rearrange("p (k t) -> p k t", k=KD),
                        scalar=S_X, in1=xt_hi[:, :, cols], op0=ALU.mult, op1=ALU.subtract).then_inc(ln2_lo, 1)
                if valid(b, g + 1):
                    i = (g + 1) % 2
                    need(dve, q_squared, s + 2)
                    nc.vector.scalar_tensor_tensor(out=q_ring[:, 1, i, :], in0=bank[5][:, :],
                                                   scalar=gains[:, 2:3], in1=q_ring[:, 0, i, :],
                                                   op0=ALU.mult, op1=ALU.subtract).then_inc(q_lo, 1)
                    need(dve, q_sumsq, s + 2)
                    nc.vector.tensor_scalar(qms[:, (g + 1) % 4, :], bank[7][:, 0:HG], 1.0 / (D * q_c2),
                                            EPS / q_c2, ALU.mult, ALU.add).then_inc(q_meansq, 1)
                if g == 0 and ln_valid(b):
                    need(dve, residual, b - 1)
                    nc.vector.bn_stats(ln2_raw[:, :], x_sb[:, b - 2, :]).then_inc(ln2_stats, 1)
                if g == 1 and ln_valid(b):
                    dve.wait_ge(ln_var, 2)
                    need(dve, ln2_stats, b - 1)
                    nc.vector.bn_aggr(ln2_small[:, 0:2], ln2_raw[:, :]).then_inc(ln2_mean, 1)
                if g == 2 and ln_valid(b):
                    need(dve, ln2_rstd, b - 1)
                    nc.vector.tensor_scalar(xn2[:, :], x_sb[:, b - 2, :], ln2_small[:, 0:1], ln2_small[:, 3:4],
                                            ALU.subtract, ALU.mult).then_inc(ln2_norm, 1)
                if valid(b, g - 3):
                    i = (g - 3) % 2
                    need(dve, u_hi, s - 2)
                    nc.vector.scalar_tensor_tensor(out=u_ring[:, 1, i, :], in0=bank[3][:, :],
                                                   scalar=S_U / (S_C * S_P), in1=u_ring[:, 0, i, :],
                                                   op0=ALU.mult, op1=ALU.subtract).then_inc(u_lo, 1)
                if g == 1 and ln_valid(b):
                    need(dve, ln2_mean, b - 1)
                    nc.vector.tensor_scalar(ln2_small[:, 2:3], ln2_small[:, 1:2], EPS, None,
                                            ALU.add).then_inc(ln2_var, 1)
                if valid(b, g + 2):
                    need(dve, kt_hi, s + 3)
                    nc.vector.scalar_tensor_tensor(out=k_ring[:, 1, g % 2, :], in0=bank[2][:, :], scalar=S_K,
                                                   in1=k_ring[:, 0, g % 2, :], op0=ALU.mult,
                                                   op1=ALU.subtract).then_inc(kt_lo, 1)
                if valid(b, g + 3):
                    need(dve, k_squared, s + 4)
                    nc.vector.reduce_sum(kss[:, (g + 3) % 4, :], k_sq[:, :, :], AX_X).then_inc(k_summed, 1)
                if g == 3 and valid(b, g - 4):
                    need(dve, out_proj, s - 3)
                    nc.vector.scalar_tensor_tensor(out=x_sb[:, b - 1, :], in0=bank[6][:, 0:DIM],
                                                   scalar=1.0 / (S_M * S_U), in1=x_sb[:, b - 1, :],
                                                   op0=ALU.mult, op1=ALU.add).then_inc(residual, 1)
                if valid(b, g + 3):
                    need(dve, k_summed, s + 4)
                    nc.vector.tensor_scalar(kms[:, (g + 3) % 4, :], kss[:, (g + 3) % 4, :], 1.0 / (D * k_c2),
                                            EPS / k_c2, ALU.mult, ALU.add).then_inc(k_meansq, 1)
                if code_valid(b):
                    c = b - 1
                    if g == 0:
                        if isinstance(b, int) and b == 1:
                            dve.wait_ge(codes_in, 16 * 9)
                        low = code_chunk(c).rearrange("p (n two) -> p n two", two=2)
                        nc.vector.tensor_copy(code16[:, :], low[:, :, 0]).then_inc(coded, 1)
                    elif g == 1:
                        need(dve, coded, c + 1)
                        signs(c, 0)
                        magnitude(c, 0)
                    elif g == 2:
                        join(c, 0)
                        signs(c, 1)
                        magnitude(c, 1)
                    else:
                        join(c, 1)
                if g == 0 and ln_valid(b):
                    c = b - 2
                    need(dve, sc_hi_done, c + 1)
                    if isinstance(b, int):
                        need(dve, decoded, c)
                    else:
                        dve.wait_ge(p_normed, s)
                    nc.vector.scalar_tensor_tensor(out=sc_lo[:, :], in0=scale_f[:, bass.ds(c * CW, CW)],
                                                   scalar=S_F * FP4_BIAS, in1=sc_hi[:, :], op0=ALU.mult,
                                                   op1=ALU.subtract).then_inc(sc_lo_done, 1)

            steps(dve, step, {-3: lambda: ln_stats(1), -1: lambda: (ln_norms(1), ln_low(1), split(4)),
                              0: lambda: (ln_low(2), ln_low(3)),
                              1: lambda: [m_low(i) for i in range(4)],
                              2: lambda: [m_low(i) for i in range(4, MG)]})
            for g in range(NG):
                step(B + 1, g)

            def chunk(half, c):
                for i in range(2):
                    u = 2 * (CH * half + c) + i
                    need(dve, gelued, u + 1)
                    nc.vector.scalar_tensor_tensor(out=pn[:, i, :], in0=bank[2 + i][:, :],
                                                   scalar=S_I / (S_F * S_X), in1=prob[:, i, :],
                                                   op0=ALU.mult, op1=ALU.mult).then_inc(hidden, 1)
                    need(dve, h_hi, u + 1)
                    nc.vector.tensor_tensor(pt_ring[:, 1, i, :], pn[:, i, :], pt_ring[:, 0, i, :],
                                            ALU.subtract).then_inc(h_lo, 1)

            def finish(half):
                for i in range(4):
                    dve.wait_ge(down, 2 * CH * (half + 1))
                    if half:
                        dve.wait_ge(out_done, 16 * 4)
                    nc.vector.scalar_tensor_tensor(out=y[:, DIM * i:DIM * i + DIM], in0=bank[4 + i][:, 0:DIM],
                                                   scalar=1.0 / (S_F * S_I), in1=x_sb[:, 4 * half + i, :],
                                                   op0=ALU.mult, op1=ALU.add).then_inc(y_done, 1)

            for half in range(2):
                chunk(half, 0)
                with dve.Fori(1, CH) as c:
                    chunk(half, c)
                finish(half)

        @block.tensor
        def _(pe):
            def three(dst, a, b, first=True, last=True):
                (a_hi, a_lo), (b_hi, b_lo) = a, b
                nc.tensor.matmul(dst, a_hi, b_hi, start=first, stop=False)
                nc.tensor.matmul(dst, a_hi, b_lo, start=False, stop=False)
                return nc.tensor.matmul(dst, a_lo, b_hi, start=False, stop=last)

            def ln_turn(i):
                pe.wait_ge(ln_norm, 2 * i + 2)
                need(pe, ln_lo, i - 1)
                for k in range(KD):
                    for t in range(2):
                        ins = nc.tensor.transpose(bank[LN_BANK[i]][:, P * (2 * k + t):P * (2 * k + t) + P],
                                                  xn1[:, DIM * (2 * i + t) + P * k:DIM * (2 * i + t) + P * k + P],
                                                  ident[:, :])
                ins.then_inc(ln_turned, 1)

            def m_product(i):
                if i < 2:
                    pe.wait_ge(ln_lo, 3 + i)
                else:
                    pe.wait_ge(m_lo_done, i - 1)
                pe.wait_ge(v_lo, 2 if i < 4 else 3)
                for t in range(2):
                    h = 2 * i + t
                    ins = three(bank[M_BANK[i]][:, DIM * t:DIM * t + DIM],
                                (wv_hi[:, CD * h:CD * h + CD], wv_lo[:, CD * h:CD * h + CD]),
                                (wo_hi[:, DIM * h:DIM * h + DIM], wo_lo[:, DIM * h:DIM * h + DIM]))
                ins.then_inc(m_prod, 1)

            def ln2_turn(b):
                need(pe, ln2_norm, b - 1)
                for k in range(KD):
                    ins = nc.tensor.transpose(bank[7][:, 256 + P * k:256 + P * k + P],
                                              xn2[:, :].rearrange("p (f two) -> p two f", two=2)[:, k, :],
                                              ident[:, :])
                ins.then_inc(ln2_turned, 1)

            pe.wait_ge(const_done, 1)
            ln_turn(0)
            pe.wait_ge(w_lo, 2)

            def step(b, g):
                s = NG * b + g
                if valid(b, g):
                    need(pe, q_lo, s + 1)
                    need(pe, kt_lo, s + 1)
                    need(pe, exps, s - 1)
                    for i in range(HG):
                        c = slice(T * i, T * i + T)
                        ins = three(bank[g % 2][:, c], (q_ring[:, 0, g % 2, c], q_ring[:, 1, g % 2, c]),
                                    (k_ring[:, 0, g % 2, c], k_ring[:, 1, g % 2, c]))
                    ins.then_inc(scores, 1)
                if valid(b, g - 2):
                    need(pe, p_normed, s - 1)
                    if valid(b, g + 1):
                        need(pe, kt_lo, s + 2)
                    else:
                        need(pe, pt_lo, s - 2)
                    for i in range(HG):
                        c = slice(T * i, T * i + T)
                        ins = nc.tensor.transpose(bank[2][:, c], pn[:, (g - 2) % 2, c], ident[:, :])
                    ins.then_inc(p_turned, 1)
                if g == 3 and ln_valid(b):
                    if valid(b, g):
                        need(pe, q_meansq, s + 1)
                    ln2_turn(b)
                if valid(b, g - 3):
                    need(pe, pt_lo, s - 2)
                    need(pe, u_lo, s - 3)
                    bb = b + (g - 3) // NG
                    c = bass.ds(bb * CD, CD)
                    i = (g - 3) % 2
                    if isinstance(b, int) and s == 3:
                        pe.wait_ge(w_lo, 5)
                        pe.wait_ge(m_lo_done, MG)
                    three(bank[3][:, :], (cx_hi[:, c], cx_lo[:, c]),
                          (pt_ring[:, 0, i, :], pt_ring[:, 1, i, :])).then_inc(mixed, 1)
                if valid(b, g - 4):
                    need(pe, u_lo, s - 3)
                    if g == 0:
                        need(pe, residual, b - 1)
                    for i in range(HG):
                        c = slice(T * i, T * i + T)
                        ins = three(bank[6][:, 0:DIM], (u_ring[:, 0, g % 2, c], u_ring[:, 1, g % 2, c]),
                                    (m_hi[:, HG * g + i, :], m_lo[:, HG * g + i, :]),
                                    g == 0 and i == 0, g == NG - 1 and i == HG - 1)
                    ins.then_inc(out_proj, 1)
                if valid(b, g + 1):
                    need(pe, q_squared, s + 2)
                    need(pe, q_meansq, s + 1)
                    if g == 3 and ln_valid(b):
                        need(pe, ln2_lo, b - 1)
                    for i in range(HG):
                        ins = nc.tensor.matmul(bank[7][:, i:i + 1], q_sq[:, T * i:T * i + T], ones[:, :],
                                               start=True, stop=True)
                    ins.then_inc(q_sumsq, 1)
                if valid(b, g + 2):
                    need(pe, k_normed, s + 3)
                    if valid(b, g - 2):
                        need(pe, pt_lo, s - 1)
                    else:
                        need(pe, kt_lo, s + 2)
                    for i in range(HG):
                        c = slice(T * i, T * i + T)
                        ins = nc.tensor.transpose(bank[2][:, c], kn[:, g % 2, c], ident[:, :])
                    ins.then_inc(k_turned, 1)
                if valid(b, g + 3):
                    need(pe, k_normed, s + 3)
                    bb, gg = b + (g + 3) // NG, (g + 3) % NG
                    c = bass.ds(bb * T, T)
                    w = slice(512 * gg, 512 * gg + 512)
                    three(bank[4][:, :], (ct_hi[:, c], ct_lo[:, c]),
                          (wk_hi[:, w], wk_lo[:, w])).then_inc(k_proj, 1)
                if valid(b, g + 2):
                    if isinstance(b, int) and s == -2:
                        pe.wait_ge(w_lo, 4)
                        pe.wait_ge(ln_lo, 1)
                    need(pe, q_lo, s + 2)
                    bb, gg = b + (g + 2) // NG, (g + 2) % NG
                    c = bass.ds(bb * T, T)
                    for i in range(HG):
                        w = slice(D * (HG * gg + i), D * (HG * gg + i) + D)
                        for k in range(KD):
                            ins = three(bank[5][:, T * i:T * i + T], (wq_hi[:, k, w], wq_lo[:, k, w]),
                                        (xt_hi[:, k, c], xt_lo[:, k, c]), k == 0, k == KD - 1)
                    ins.then_inc(q_proj, 1)

            steps(pe, step, {-1: lambda: ln_turn(1),
                             0: lambda: (ln_turn(2), ln_turn(3)),
                             1: lambda: [m_product(i) for i in range(4)],
                             2: lambda: [m_product(i) for i in range(4, MG)]})

            def gate_up_proj(half, c, i):
                u = 2 * (CH * half + c) + i
                need(pe, hidden, u - 1)
                for mat in range(2):
                    for k in range(KD):
                        w = bass.ds(c * 1536 + (768 * k + 256 * mat + P * i), P)
                        t = slice(HT * half, HT * half + HT)
                        ins = three(bank[2 * mat + i][:, :], (wf_hi[:, w], wf_lo[:, w]),
                                    (xt_hi[:, k, t], xt_lo[:, k, t]), k == 0, k == KD - 1)
                ins.then_inc(gate_up, 1)

            def down_proj(half, c, i, first=False, last=False):
                u = 2 * (CH * half + c) + i
                need(pe, h_lo, u + 1)
                w = bass.ds(c * 1536 + (768 * i + 512), DIM)
                for t in range(4):
                    a = slice(P * t, P * t + P)
                    ins = three(bank[4 + t][:, 0:DIM], (pt_ring[:, 0, i, a], pt_ring[:, 1, i, a]),
                                (wf_hi[:, w], wf_lo[:, w]), first, last)
                ins.then_inc(down, 1)

            for half in range(2):
                if half:
                    pe.wait_ge(y_done, 4)
                    pe.wait_ge(ln2_lo, B)
                else:
                    pe.wait_ge(ln2_lo, B - 1)
                    pe.wait_ge(decoded, 1)
                gate_up_proj(half, 0, 0)
                gate_up_proj(half, 0, 1)
                if half == 0:
                    ln2_turn(B + 1)
                def both(c, first=False):
                    if half == 0:
                        need(pe, decoded, c + 1)
                    for i in range(2):
                        gate_up_proj(half, c, i)
                        if half == 0 and i == 0:
                            pe.wait_ge(ln2_lo, B)
                        down_proj(half, c - 1, i, first=first and i == 0)

                both(1, first=True)
                with pe.Fori(2, CH) as c:
                    both(c)
                down_proj(half, CH - 1, 0)
                down_proj(half, CH - 1, 1, last=True)


def kernel(**inputs):
    import numpy as np
    import concourse.bacc as bacc
    from concourse.bass_utils import run_bass_kernel_spmd

    a = {n: np.asarray(v) for n, v in inputs.items()}

    def columns(w):
        return w.T.reshape(w.shape[1], CH, P, 2).transpose(0, 1, 3, 2).reshape(w.shape[1], CH, 2 * P)

    dp, ds = a["L0_ffn_down_W_packed"], a["L0_ffn_down_scales"]
    down_codes = dp.T.reshape(CH, P, DIM).transpose(1, 0, 2)
    down_scales = ds.T.reshape(CH, 2 * P // BLK, DIM).transpose(1, 0, 2)
    codes = np.stack([columns(a["L0_ffn_gate_W_packed"]), columns(a["L0_ffn_up_W_packed"]), down_codes], axis=2)
    scales = np.stack([columns(a["L0_ffn_gate_scales"]), columns(a["L0_ffn_up_scales"]), down_scales], axis=2)
    arrays = {
        "x": a["x"].reshape(B * T, DIM),
        "ctx": a["ctx_1024"].reshape(B * T, CD),
        "ctx_t": a["ctx_1024"].reshape(B * T, CD).T,
        "wq": a["L0_xattn_Wq"],
        "wk": a["L0_xattn_Wk"],
        "wv_t": a["L0_xattn_Wv"].reshape(CD, H, D).transpose(2, 1, 0).reshape(D, H * CD),
        "wo": a["L0_xattn_Wo"],
        "gq": a["L0_xattn_gq"].reshape(D, 1),
        "gk": a["L0_xattn_gk"].reshape(D, 1),
        "packed": codes.reshape(P, CH * 3 * DIM),
        "scales": scales.reshape(8, CH * 3 * DIM),
    }
    arrays = {n: np.ascontiguousarray(v) for n, v in arrays.items()}
    nc = bacc.Bacc("TRN2", target_bir_lowering=False, num_devices=1)
    args = [nc.dram_tensor(n, v.shape, mybir.dt.from_np(v.dtype), kind="ExternalInput").ap()
            for n, v in arrays.items()]
    out = nc.dram_tensor("out", (B * T, DIM), F32, kind="ExternalOutput").ap()
    xattn_ffn(nc, *args, out)
    r = run_bass_kernel_spmd(nc, [arrays], core_ids=[0])
    return r.results[0]["out"].reshape(B, T, DIM)
```

```python
from contextlib import ExitStack

import concourse.bass as bass
from concourse import mybir
from concourse.alu_op_type import AluOpType as ALU

ACT = mybir.ActivationFunctionType
AX_X = mybir.AxisListType.X
F32 = mybir.dt.float32
F16 = mybir.dt.float16
BF16 = mybir.dt.bfloat16
I32 = mybir.dt.int32
U16 = mybir.dt.uint16

P = 128
B, T, DIM = 8, 128, 256
CD = 128
H, D = 16, 128
INNER = H * D
MLP = 2048
BLK = 32
KD = DIM // P
HG = 4
NG = H // HG
NS = B * NG
CH = MLP // (2 * P)
HT = 512
EPS = 1e-5

S_X = 2.0 ** 8
S_W = 2.0 ** 10
S_C = 2.0 ** 7
S_M = 2.0 ** 10
S_Q = 2.0 ** 6
S_K = 2.0 ** 8
S_P = 2.0 ** 10
S_U = 2.0 ** 7
S_F = 2.0 ** 5
S_I = 2.0 ** 3
FP4_BIAS = 2.0 ** 14


def part(view, n, shape):
    names = "abcd"[:len(shape)]
    sizes = dict(zip(names, shape))
    return view[:, 0:n].rearrange(f"p ({' '.join(names)}) -> p {' '.join(names)}", **sizes)


def need(eng, sem, value):
    if not isinstance(value, int) or value > 0:
        eng.wait_ge(sem, value)


def xattn_ffn(nc, x, ctx, ctx_t, wq, wk, wv_t, wo, gq, gk, packed, scales, out):
    with ExitStack() as stack:
        def sb(name, shape, dt):
            return stack.enter_context(nc.sbuf_tensor(name, shape, dt))

        def sem(name):
            return stack.enter_context(nc.semaphore(name))

        bank = [stack.enter_context(nc.psum_tensor(f"bank{i}", [P, 512], F32)) for i in range(8)]

        x_sb = sb("x_sb", [P, B, DIM], F32)
        xt_hi = sb("xt_hi", [P, KD, B * T], F16)
        xt_lo = sb("xt_lo", [P, KD, B * T], F16)
        wq_hi = sb("wq_hi", [P, KD, INNER], F16)
        wq_lo = sb("wq_lo", [P, KD, INNER], F16)
        wk_hi = sb("wk_hi", [P, INNER], F16)
        wk_lo = sb("wk_lo", [P, INNER], F16)
        ct_hi = sb("ct_hi", [P, B * T], F16)
        ct_lo = sb("ct_lo", [P, B * T], F16)
        cx_hi = sb("cx_hi", [P, B * CD], F16)
        cx_lo = sb("cx_lo", [P, B * CD], F16)
        m_hi = sb("m_hi", [P, H, DIM], F16)
        m_lo = sb("m_lo", [P, H, DIM], F16)
        ident = sb("ident", [P, P], F32)
        ones = sb("ones", [P, 1], F32)
        mhalf = sb("mhalf", [P, B], F32)
        gains = sb("gains", [P, 3], F32)

        NF = CH * 3 * DIM
        stage = sb("stage", [P, 2 * NF], F32)
        wq_f = part(stage[:, 0:4096], 4096, (KD, INNER))
        wk_f = stage[:, 4096:6144]
        wv_f = stage[:, 6144:8192]
        wo_f = stage[:, 8192:12288]
        codes = stage[:, 0:NF].bitcast(I32)
        scale_f = stage[:, NF:2 * NF]
        ffn = sb("ffn", [P, 4 * NF], F16)
        wf_hi = ffn[:, 0:2 * NF]
        wf_lo = ffn[:, 2 * NF:4 * NF]
        xn1 = ffn[:, 0:4096].bitcast(F32)
        ct_f = ffn[:, 4096:6144].bitcast(F32)
        cx_f = ffn[:, 6144:8192].bitcast(F32)

        q_ring = sb("q_ring", [P, 2, 2, 512], F16)
        k_ring = sb("k_ring", [P, 2, 2, 512], F16)
        u_ring = sb("u_ring", [P, 2, 2, 512], F16)
        pt_ring = sb("pt_ring", [P, 2, 2, 512], F16)
        q_sq = sb("q_sq", [P, 512], F32)
        k_sq = sb("k_sq", [P, HG, T], F32)
        kn = sb("kn", [P, 2, 512], F32)
        prob = sb("prob", [P, 2, 512], F32)
        pn = sb("pn", [P, 2, 512], F32)
        kms = sb("kms", [P, 4, HG], F32)
        kss = sb("kss", [P, 4, HG], F32)
        k_rstd = sb("k_rstd", [P, 4, HG], F32)
        qms = sb("qms", [P, 4, HG], F32)
        q_rstd = sb("q_rstd", [P, 4, HG], F32)
        top = sb("top", [P, 4, HG], F32)
        neg_top = sb("neg_top", [P, 4, HG], F32)
        den = sb("den", [P, 4, HG], F32)
        rden = sb("rden", [P, 4, HG], F32)
        stats = sb("stats", [P, B, 6], F32)
        mean_var = sb("mean_var", [P, B, 2], F32)
        var_eps = sb("var_eps", [P, B], F32)
        rstd = sb("rstd", [P, B], F32)
        ln2_raw = sb("ln2_raw", [P, 6], F32)
        ln2_small = sb("ln2_small", [P, 4], F32)
        xn2 = sb("xn2", [P, DIM], F32)

        CW = 3 * DIM
        code16 = sb("code16", [P, CW], U16)
        sign16 = sb("sign16", [P, CW], U16)
        sc_hi = sb("sc_hi", [P, CW], BF16)
        sc_lo = sb("sc_lo", [P, CW], F16)
        y = kn[:, :, :].rearrange("p a n -> p (a n)")

        def code_chunk(c):
            return codes[:, bass.ds(c * CW, CW)].bitcast(U16)

        x_in = [sem(f"x_in{i}") for i in range(2)]
        W_NAMES = ("ct_a", "wk0", "wq0", "wk1", "wq1", "wk2", "wq2", "wk3", "wq3", "cx_a", "ct_b", "cx_b",
                   "wv", "wo0", "wo1")
        w_in = {n: sem(f"{n}_in") for n in W_NAMES}
        gains_in, codes_in, scales_in = sem("gains_in"), sem("codes_in"), sem("scales_in")
        out_done = sem("out_done")
        const_done, gain_done = sem("const_done"), sem("gain_done")
        dve_self = sem("dve_self")
        pool_self = sem("pool_self")
        w_hi = sem("w_hi")
        lo_done = {n: sem(f"{n}_lo_done") for n in W_NAMES[:-3]}
        ln_var, ln_rstd, ln_norm = sem("ln_var"), sem("ln_rstd"), sem("ln_norm")
        ln_turned, ln_hi, ln_lo = sem("ln_turned"), sem("ln_hi"), sem("ln_lo")
        m_prod, m_hi_done, m_lo_done = sem("m_prod"), sem("m_hi_done"), sem("m_lo_done")
        k_proj, k_turned, q_proj, q_sumsq = sem("k_proj"), sem("k_turned"), sem("q_proj"), sem("q_sumsq")
        scores, p_turned, mixed, out_proj = sem("scores"), sem("p_turned"), sem("mixed"), sem("out_proj")
        k_squared, kt_hi, q_squared = sem("k_squared"), sem("kt_hi"), sem("q_squared")
        exps, pt_hi = sem("exps"), sem("pt_hi")
        k_summed, k_meansq, k_normed, kt_lo = sem("k_summed"), sem("k_meansq"), sem("k_normed"), sem("kt_lo")
        q_meansq, q_lo, topped, neg_topped = sem("q_meansq"), sem("q_lo"), sem("topped"), sem("neg_topped")
        rden_done, pt_lo, u_hi, u_lo = sem("rden_done"), sem("pt_lo"), sem("u_hi"), sem("u_lo")
        residual = sem("residual")
        k_rstd_done, q_rstd_done, p_normed = sem("k_rstd_done"), sem("q_rstd_done"), sem("p_normed")
        coded, signed, joined = sem("coded"), sem("signed"), sem("joined")
        sc_hi_done, sc_lo_done = sem("sc_hi_done"), sem("sc_lo_done")
        hi_decoded, decoded = sem("hi_decoded"), sem("decoded")
        ln2_stats, ln2_mean, ln2_var, ln2_rstd = (sem(f"ln2_{n}") for n in ("stats", "mean", "var", "rstd"))
        ln2_norm, ln2_turned, ln2_hi, ln2_lo = (sem(f"ln2_{n}") for n in ("norm", "turned", "hi", "lo"))
        gate_up, gelued, hidden, h_hi, h_lo = (sem(n) for n in ("gate_up", "gelued", "hidden", "h_hi", "h_lo"))
        down, y_done = sem("down"), sem("y_done")

        def head_piece(w, g):
            return w[..., 512 * g:512 * g + 512]

        splits = [("ct_a", ct_f[:, 0:2 * T], ct_hi[:, 0:2 * T], ct_lo[:, 0:2 * T], S_C)]
        for g in range(NG):
            splits.append((f"wk{g}", head_piece(wk_f, g), head_piece(wk_hi, g), head_piece(wk_lo, g), S_W))
            splits.append((f"wq{g}", head_piece(wq_f, g), head_piece(wq_hi, g), head_piece(wq_lo, g), S_W))
        splits += [("cx_a", cx_f[:, 0:2 * CD], cx_hi[:, 0:2 * CD], cx_lo[:, 0:2 * CD], S_C),
                   ("ct_b", ct_f[:, 2 * T:], ct_hi[:, 2 * T:], ct_lo[:, 2 * T:], S_C),
                   ("cx_b", cx_f[:, 2 * CD:], cx_hi[:, 2 * CD:], cx_lo[:, 2 * CD:], S_C)]
        order = {piece[0]: n for n, piece in enumerate(splits)}
        GPSIMD_LOWS = ("wq2", "wq3")
        MG = H // 2

        def valid(b, off):
            return not isinstance(b, int) or 0 <= NG * b + off < NS

        def ln_valid(b):
            return not isinstance(b, int) or 2 <= b < B + 2

        def late_q_sums(b, g):
            return g == 3 and ln_valid(b)

        def code_valid(b):
            return not isinstance(b, int) or 1 <= b < B + 1

        def steps(eng, step, behind):
            for s in range(-3, 2 * NG):
                step(s // NG, s % NG)
                behind(s)
            with eng.Fori(2, B - 1) as b:
                for g in range(NG):
                    step(b, g)
            for s in range(NS - NG, NS + 4):
                step(s // NG, s % NG)
                behind(s)

        LN_PARTS = [(0, 2), (2, 4), (4, 6), (6, 8)]

        def ln_view(n):
            if n == 0:
                return bank[3][:, :].rearrange("p (k t) -> p k t", k=KD), slice(0, 2 * T)
            return bank[7][:, 256:512].rearrange("p (k t) -> p k t", k=KD), slice(T * (n + 1), T * (n + 2))

        M_BANK = [6, 3, 6, 3, 6, 3, 6, 3]

        GATE, UP, SUM = (4, 5), (0, 1), (2, 3, 6, 7)

        def beside_attention(half, c):
            return half == 0 and isinstance(c, int) and c == 0

        def ln2_view(b):
            v = bank[GATE[0]][:, 0:256] if isinstance(b, int) and b == B + 1 else bank[7][:, 256:512]
            return v.rearrange("p (k t) -> p k t", k=KD)

        def downs(half, n):
            return n + 3 * half

        block = stack.enter_context(nc.Block())

        @block.sync
        def _(sp):
            x_v = x.rearrange("(b t) n -> t b n", t=T)
            wo_v = wo.rearrange("(h d) n -> d h n", d=D)
            wq_v = wq.rearrange("(k p) n -> p k n", p=P)

            def load(name, dst, src):
                sp.dma_start(dst, src).then_inc(w_in[name], 16)

            def load_wk(g):
                load(f"wk{g}", head_piece(wk_f, g), head_piece(wk, g))

            def load_wq(g):
                load(f"wq{g}", head_piece(wq_f, g), head_piece(wq_v, g))

            def load_wo(i):
                load(f"wo{i}", part(wo_f[:, 2048 * i:2048 * i + 2048], 2048, (8, DIM)),
                     wo_v[:, 8 * i:8 * i + 8, :])

            load("ct_a", ct_f[:, 0:2 * T], ctx_t[:, 0:2 * T])
            load_wk(0)
            load_wq(0)
            load_wk(1)
            load_wq(1)
            load_wk(2)
            load("wv", wv_f, wv_t)
            load_wo(0)
            load_wq(2)
            load_wk(3)
            load_wq(3)
            sp.dma_start(x_sb[:, 2:B, :], x_v[:, 2:B, :]).then_inc(x_in[1], 16)
            cx_v = ctx.rearrange("(b t) c -> t b c", t=T)
            load("cx_a", part(cx_f, 2 * CD, (2, CD)), cx_v[:, 0:2, :])
            load_wo(1)
            load("ct_b", ct_f[:, 2 * T:], ctx_t[:, 2 * T:])
            load("cx_b", part(cx_f[:, 2 * CD:], (B - 2) * CD, (B - 2, CD)), cx_v[:, 2:B, :])
            for g in range(NG):
                sp.wait_ge(lo_done[f"wk{g}"], 1)
                sp.wait_ge(lo_done[f"wq{g}"], 1)
            sp.dma_start(codes, packed).then_inc(codes_in, 16)
            sp.wait_ge(m_prod, MG)
            for i in range(8):
                sp.dma_start(scale_f[16 * i:16 * i + 16, :],
                             scales[i:i + 1, :].broadcast_to([16, NF])).then_inc(scales_in, 16)
            out_v = out.rearrange("(b t) n -> t b n", t=T)
            for half in range(2):
                for i in range(4):
                    sp.wait_ge(y_done, 4 * half + i + 1)
                    sp.dma_start(out_v[:, 4 * half + i, :], y[:, DIM * i:DIM * i + DIM]).then_inc(out_done, 16)
            sp.wait_ge(out_done, 16 * B)

        @block.gpsimd
        def _(pool):
            nc.gpsimd.memset(ident[:, :], 0.0).then_inc(pool_self, 1)
            nc.gpsimd.memset(mhalf[:, :], -0.5).then_inc(pool_self, 1)
            nc.gpsimd.memset(ones[:, :], 1.0).then_inc(pool_self, 1)
            pool.wait_ge(pool_self, 3)
            nc.gpsimd.affine_select(out=ident[:, :], in_=ident[:, :], compare_op=ALU.not_equal, fill=1.0,
                                    base=0, pattern=[[-1, P]], channel_multiplier=1).then_inc(const_done, 1)

            def ln_root(n):
                pool.wait_ge(ln_var, n + 1)
                a, b = LN_PARTS[n]
                nc.gpsimd.tensor_tensor(rstd[:, a:b], var_eps[:, a:b], mhalf[:, a:b], ALU.pow).then_inc(ln_rstd, 1)

            def ln_norm_tile(t):
                pool.wait_ge(ln_rstd, t // 2 + 1)
                nc.gpsimd.tensor_scalar(xn1[:, DIM * t:DIM * t + DIM], x_sb[:, t, :], mean_var[:, t, 0:1],
                                        rstd[:, t:t + 1], ALU.subtract, ALU.mult).then_inc(ln_norm, 1)

            def weights(b, n):
                c = b - 2
                w, sc = ((wf_hi, sc_hi), (wf_lo, sc_lo))[n // 3]
                if n == 0:
                    pool.wait_ge(codes_in, 16)
                    need(pool, joined, 2 * c + 2)
                    need(pool, sc_hi_done, c + 1)
                if n == 3:
                    need(pool, sc_lo_done, c + 1)
                k = slice(DIM * (n % 3), DIM * (n % 3) + DIM)
                mags = code_chunk(c).bitcast(F16).rearrange("p (two n) -> p two n", two=2)
                dst = w[:, bass.ds(c * 2 * CW, 2 * CW)].rearrange("p (two n) -> p two n", two=2)
                ins = nc.gpsimd.tensor_tensor(dst[:, :, k], mags[:, :, k],
                                              sc[:, k].unsqueeze(1).broadcast_to([P, 2, DIM]), ALU.mult)
                if n == 2:
                    ins.then_inc(hi_decoded, 1)
                if n == 5:
                    ins.then_inc(decoded, 1)

            def ln2_root(b):
                need(pool, ln2_var, b - 1)
                nc.gpsimd.tensor_tensor(ln2_small[:, 3:4], ln2_small[:, 2:3], mhalf[:, 0:1],
                                        ALU.pow).then_inc(ln2_rstd, 1)

            PIECES = ((0, 1), (2,), (3, 4), (5,))

            ln_root(0)

            def step(b, g):
                s = NG * b + g
                if valid(b, g - 1):
                    j, i, q = s - 1, (g - 1) % 2, (g - 1) % 4
                    need(pool, rden_done, j + 1)
                    need(pool, p_turned, j - 1)
                    nc.gpsimd.tensor_tensor(
                        pn[:, i, :].rearrange("p (h k) -> p h k", h=HG),
                        prob[:, i, :].rearrange("p (h k) -> p h k", h=HG),
                        rden[:, q, :].unsqueeze(2).broadcast_to([P, HG, T]), ALU.mult).then_inc(p_normed, 1)
                if valid(b, g + 1):
                    need(pool, q_meansq, s + 2)
                    nc.gpsimd.tensor_tensor(q_rstd[:, (g + 1) % 4, :], qms[:, (g + 1) % 4, :],
                                            mhalf[:, 0:HG], ALU.pow).then_inc(q_rstd_done, 1)
                if valid(b, g + 3):
                    need(pool, k_meansq, s + 4)
                    nc.gpsimd.tensor_tensor(k_rstd[:, (g + 3) % 4, :], kms[:, (g + 3) % 4, :],
                                            mhalf[:, 0:HG], ALU.pow).then_inc(k_rstd_done, 1)
                if g == 1 and ln_valid(b):
                    ln2_root(b)
                if ln_valid(b):
                    for n in PIECES[g]:
                        weights(b, n)

            def low(piece):
                name, src, hi, lo, _ = splits[order[piece]]
                pool.wait_ge(w_hi, order[piece] + 1)
                nc.gpsimd.tensor_tensor(lo, src, hi, ALU.subtract).then_inc(lo_done[name], 1)

            def behind(s):
                if s == -2:
                    ln_root(1)
                    low("wq2")
                if s == -1:
                    low("wq3")
                if s in (2, 4):
                    ln_root(s // 2 + 1)
                if 0 <= s < B - 2:
                    ln_norm_tile(s + 2)
                if s == 2 * NG - 1:
                    pool.wait_ge(ln_turned, B - 1)

            steps(pool, step, behind)
            ln2_root(B + 1)
            for n in range(6):
                weights(B + 1, n)

        @block.scalar
        def _(act):
            act.dma_start(x_sb[:, 0:2, :], x.rearrange("(b t) n -> t b n", t=T)[:, 0:2, :]).then_inc(x_in[0], 16)
            act.dma_start(gains[:, 0:1], gq).then_inc(gains_in, 16)
            act.dma_start(gains[:, 1:2], gk).then_inc(gains_in, 16)

            def split(piece):
                name, src, hi, lo, scale = splits[order[piece]]
                act.wait_ge(w_in[name], 16)
                ins = nc.scalar.activation(hi, src, ACT.Copy, scale=scale)
                if name in GPSIMD_LOWS:
                    ins = nc.scalar.activation(src, src, ACT.Copy, scale=scale)
                ins.then_inc(w_hi, 1)

            def ln_high(n):
                act.wait_ge(ln_turned, n + 1)
                src, t = ln_view(n)
                nc.scalar.activation(xt_hi[:, :, t], src, ACT.Copy, scale=S_X).then_inc(ln_hi, 1)

            def m_high(i):
                act.wait_ge(m_prod, i + 1)
                nc.scalar.activation(m_hi[:, 2 * i:2 * i + 2, :],
                                     bank[M_BANK[i]][:, :].rearrange("p (h n) -> p h n", h=2),
                                     ACT.Copy, scale=S_M).then_inc(m_hi_done, 1)

            for piece in ("ct_a", "wk0", "wq0", "wk1"):
                split(piece)

            def ln2_high(b):
                need(act, ln2_turned, b - 1)
                nc.scalar.activation(xt_hi[:, :, bass.ds((b - 2) * T, T)], ln2_view(b), ACT.Copy,
                                     scale=S_X).then_inc(ln2_hi, 1)

            def gelu(half, c, i):
                u = 2 * (CH * half + c) + i
                need(act, gate_up, u + 1)
                need(act, hidden, u - 1)
                if beside_attention(half, c):
                    act.wait_ge(p_normed, NS - 1 + i)
                nc.scalar.activation(prob[:, i, :], bank[GATE[i]][:, :], ACT.Gelu_apprx_tanh,
                                     scale=1.0 / (S_F * S_X)).then_inc(gelued, 1)

            def hidden_high(half, c, i):
                u = 2 * (CH * half + c) + i
                need(act, hidden, u + 1)
                if beside_attention(half, c):
                    act.wait_ge(mixed, NS - 1 + i)
                else:
                    act.wait_ge(down, downs(half, u - 1))
                nc.scalar.activation(pt_ring[:, 0, i, :], pn[:, i, :], ACT.Copy).then_inc(h_hi, 1)

            def tile(half, c, i):
                gelu(half, c, i)
                hidden_high(half, c, i)

            def step(b, g):
                s = NG * b + g
                if valid(b, g - 2):
                    need(act, p_turned, s - 1)
                    nc.scalar.activation(pt_ring[:, 0, (g - 2) % 2, :], bank[2][:, :], ACT.Copy,
                                         scale=S_P).then_inc(pt_hi, 1)
                if g == 3 and ln_valid(b):
                    ln2_high(b)
                if valid(b, g - 3):
                    need(act, mixed, s - 2)
                    nc.scalar.activation(u_ring[:, 0, (g - 3) % 2, :], bank[3][:, :], ACT.Copy,
                                         scale=S_U / (S_C * S_P)).then_inc(u_hi, 1)
                if valid(b, g):
                    need(act, neg_topped, s + 1)
                    need(act, p_normed, s - 1)
                    for i in range(HG):
                        ins = nc.scalar.activation(prob[:, g % 2, T * i:T * i + T],
                                                   bank[g % 2][:, T * i:T * i + T], ACT.Exp,
                                                   scale=q_rstd[:, g, i:i + 1], bias=neg_top[:, g, i:i + 1],
                                                   accum_out=den[:, g, i:i + 1])
                    ins.then_inc(exps, 1)
                if valid(b, g + 2):
                    need(act, k_turned, s + 3)
                    nc.scalar.activation(k_ring[:, 0, g % 2, :], bank[2][:, :], ACT.Copy,
                                         scale=S_K).then_inc(kt_hi, 1)
                if valid(b, g + 3):
                    need(act, k_proj, s + 4)
                    need(act, k_summed, s + 3)
                    nc.scalar.activation(k_sq[:, :, :].rearrange("p h d -> p (h d)"), bank[4][:, :],
                                         ACT.Square, scale=1.0 / (S_W * S_C)).then_inc(k_squared, 1)
                if isinstance(b, int) and -2 <= s < MG // 2 - 2:
                    m_high(2 * s + 4)
                    m_high(2 * s + 5)
                if valid(b, g + 2):
                    need(act, q_proj, s + 3)
                    nc.scalar.activation(q_ring[:, 0, g % 2, :], bank[5][:, :], ACT.Copy,
                                         scale=gains[:, 2:3])
                    nc.scalar.activation(q_sq[:, :], bank[5][:, :], ACT.Square,
                                         scale=1.0 / (S_W * S_X)).then_inc(q_squared, 1)
                if g == 2 and code_valid(b):
                    if isinstance(b, int) and b == 1:
                        act.wait_ge(scales_in, 16 * 8)
                    need(act, hi_decoded, b - 1)
                    nc.scalar.activation(sc_hi[:, :], scale_f[:, bass.ds((b - 1) * CW, CW)], ACT.Copy,
                                         scale=S_F * FP4_BIAS).then_inc(sc_hi_done, 1)

            def behind(s):
                if s == -3:
                    ln_high(0)
                    split("wq1")
                    split("wk2")
                    act.wait_ge(gain_done, 1)
                if s == -2:
                    split("wq2")
                    split("wk3")
                if s == -1:
                    split("wq3")
                if s == 0:
                    split("cx_a")
                if 1 <= s < B - 1:
                    ln_high(s)
                if s == 2:
                    split("ct_b")
                if s == 3:
                    split("cx_b")
                if s == NS + 1:
                    gelu(0, 0, 0)
                if s == NS + 2:
                    hidden_high(0, 0, 0)
                    gelu(0, 0, 1)
                if s == NS + 3:
                    hidden_high(0, 0, 1)

            steps(act, step, behind)
            for half in range(2):
                if half:
                    tile(half, 0, 0)
                    tile(half, 0, 1)
                    tile(half, 1, 0)
                    tile(half, 1, 1)
                else:
                    tile(0, 1, 0)
                    gelu(0, 1, 1)
                    ln2_high(B + 1)
                    hidden_high(0, 1, 1)
                with act.Fori(2, CH) as c:
                    tile(half, c, 0)
                    tile(half, c, 1)

        @block.vector
        def _(dve):
            link_n = [0]

            def link(ins):
                link_n[0] += 1
                ins.then_inc(dve_self, 1)
                dve.wait_ge(dve_self, link_n[0])

            def ln_stats(n):
                a, b = LN_PARTS[n]
                dve.wait_ge(x_in[min(n, 1)], 16)
                for i in range(a, b):
                    ins = nc.vector.bn_stats(stats[:, i, :], x_sb[:, i, :])
                link(ins)
                for i in range(a, b):
                    ins = nc.vector.bn_aggr(mean_var[:, i, :], stats[:, i, :])
                link(ins)
                nc.vector.tensor_scalar(var_eps[:, a:b], mean_var[:, a:b, 1], EPS, None, ALU.add).then_inc(ln_var, 1)

            def ln_norm_tile(t):
                dve.wait_ge(ln_rstd, 1)
                nc.vector.tensor_scalar(xn1[:, DIM * t:DIM * t + DIM], x_sb[:, t, :], mean_var[:, t, 0:1],
                                        rstd[:, t:t + 1], ALU.subtract, ALU.mult).then_inc(ln_norm, 1)

            def ln_low(n):
                dve.wait_ge(ln_hi, n + 1)
                src, t = ln_view(n)
                nc.vector.scalar_tensor_tensor(out=xt_lo[:, :, t], in0=src, scalar=S_X, in1=xt_hi[:, :, t],
                                               op0=ALU.mult, op1=ALU.subtract).then_inc(ln_lo, 1)

            def split(piece):
                name, src, hi, lo, scale = splits[order[piece]]
                dve.wait_ge(w_hi, order[piece] + 1)
                nc.vector.scalar_tensor_tensor(out=lo, in0=src, scalar=scale, in1=hi, op0=ALU.mult,
                                               op1=ALU.subtract).then_inc(lo_done[name], 1)

            def m_low(i):
                dve.wait_ge(m_hi_done, i + 1)
                nc.vector.scalar_tensor_tensor(
                    out=m_lo[:, 2 * i:2 * i + 2, :], in0=bank[M_BANK[i]][:, :].rearrange("p (h n) -> p h n", h=2),
                    scalar=S_M, in1=m_hi[:, 2 * i:2 * i + 2, :], op0=ALU.mult,
                    op1=ALU.subtract).then_inc(m_lo_done, 1)

            ln_stats(0)
            split("ct_a")
            ln_norm_tile(0)
            ln_norm_tile(1)
            split("wk0")
            split("wq0")
            dve.wait_ge(gains_in, 32)
            nc.vector.scalar_tensor_tensor(out=gains[:, 2:3], in0=gains[:, 0:1], scalar=S_Q / (S_W * S_X),
                                           in1=gains[:, 1:2], op0=ALU.mult, op1=ALU.mult).then_inc(gain_done, 1)

            q_c2 = (float(D) ** -0.5 / (S_Q * S_K)) ** 2
            k_c2 = (1.0 / (S_W * S_C)) ** 2

            def signs(b, n):
                need(dve, joined, 2 * b + n)
                mask, up = ((0x08, 12), (0x80, 8))[n]
                nc.vector.tensor_scalar(sign16[:, :], code16[:, :], mask, up, ALU.bitwise_and,
                                        ALU.logical_shift_left)

            def magnitude(b, n):
                mask, up = ((0x07, 9), (0x70, 5))[n]
                nc.vector.tensor_scalar(code_chunk(b)[:, CW * n:CW * n + CW], code16[:, :], mask, up,
                                        ALU.bitwise_and, ALU.logical_shift_left).then_inc(signed, 1)

            def join(b, n):
                need(dve, signed, 2 * b + n + 1)
                dst = code_chunk(b)[:, CW * n:CW * n + CW]
                nc.vector.tensor_tensor(dst, dst, sign16[:, :], ALU.bitwise_or).then_inc(joined, 1)

            def ln2_low(b):
                need(dve, ln2_hi, b - 1)
                cols = bass.ds((b - 2) * T, T)
                nc.vector.scalar_tensor_tensor(out=xt_lo[:, :, cols], in0=ln2_view(b), scalar=S_X,
                                               in1=xt_hi[:, :, cols], op0=ALU.mult,
                                               op1=ALU.subtract).then_inc(ln2_lo, 1)

            def hide(half, c, i):
                u = 2 * (CH * half + c) + i
                need(dve, gelued, u + 1)
                if beside_attention(half, c):
                    dve.wait_ge(p_turned, NS - 1 + i)
                nc.vector.scalar_tensor_tensor(out=pn[:, i, :], in0=bank[UP[i]][:, :],
                                               scalar=S_I / (S_F * S_X), in1=prob[:, i, :],
                                               op0=ALU.mult, op1=ALU.mult).then_inc(hidden, 1)

            def hidden_low(half, c, i):
                u = 2 * (CH * half + c) + i
                need(dve, h_hi, u + 1)
                nc.vector.tensor_tensor(pt_ring[:, 1, i, :], pn[:, i, :], pt_ring[:, 0, i, :],
                                        ALU.subtract).then_inc(h_lo, 1)

            def tile(half, c, i):
                hide(half, c, i)
                hidden_low(half, c, i)

            def normalise_keys(b, g):
                if not valid(b, g + 2):
                    return
                s = NG * b + g
                need(dve, k_rstd_done, s + 3)
                need(dve, k_turned, s + 1)
                nc.vector.tensor_tensor(
                    kn[:, g % 2, :].rearrange("p (h d) -> p h d", h=HG),
                    bank[4][:, :].rearrange("p (h d) -> p h d", h=HG),
                    k_rstd[:, (g + 2) % 4, :].unsqueeze(2).broadcast_to([P, HG, D]),
                    ALU.mult).then_inc(k_normed, 1)

            def query_means(b, g):
                if not valid(b, g + 1):
                    return
                s = NG * b + g
                need(dve, q_sumsq, s + 2)
                nc.vector.tensor_scalar(qms[:, (g + 1) % 4, :], bank[7][:, 0:HG], 1.0 / (D * q_c2),
                                        EPS / q_c2, ALU.mult, ALU.add).then_inc(q_meansq, 1)

            def step(b, g):
                s = NG * b + g
                start = isinstance(b, int) and b <= 0
                if valid(b, g):
                    need(dve, scores, s + 1)
                    nc.vector.reduce_max(top[:, g, :], bank[g % 2][:, :].rearrange("p (h k) -> p h k", h=HG),
                                         AX_X).then_inc(topped, 1)
                if valid(b, g - 1):
                    need(dve, exps, s)
                    nc.vector.reciprocal(rden[:, (g - 1) % 4, :], den[:, (g - 1) % 4, :]).then_inc(rden_done, 1)
                if valid(b, g):
                    need(dve, topped, s + 1)
                    need(dve, q_rstd_done, s + 1)
                    nc.vector.scalar_tensor_tensor(out=neg_top[:, g, :], in0=top[:, g, :], scalar=-1.0,
                                                   in1=q_rstd[:, g, :], op0=ALU.mult,
                                                   op1=ALU.mult).then_inc(neg_topped, 1)
                if not start:
                    normalise_keys(b, g)
                if valid(b, g - 2):
                    need(dve, pt_hi, s - 1)
                    i = (g - 2) % 2
                    nc.vector.scalar_tensor_tensor(out=pt_ring[:, 1, i, :], in0=bank[2][:, :], scalar=S_P,
                                                   in1=pt_ring[:, 0, i, :], op0=ALU.mult,
                                                   op1=ALU.subtract).then_inc(pt_lo, 1)
                if g == 3 and ln_valid(b):
                    ln2_low(b)
                if valid(b, g + 1):
                    i = (g + 1) % 2
                    need(dve, q_squared, s + 2)
                    nc.vector.scalar_tensor_tensor(out=q_ring[:, 1, i, :], in0=bank[5][:, :],
                                                   scalar=gains[:, 2:3], in1=q_ring[:, 0, i, :],
                                                   op0=ALU.mult, op1=ALU.subtract).then_inc(q_lo, 1)
                if not late_q_sums(b, g):
                    query_means(b, g)
                if g == 0 and ln_valid(b):
                    need(dve, residual, b - 1)
                    nc.vector.bn_stats(ln2_raw[:, :], x_sb[:, b - 2, :]).then_inc(ln2_stats, 1)
                if g == 1 and ln_valid(b):
                    dve.wait_ge(ln_var, 2)
                    need(dve, ln2_stats, b - 1)
                    nc.vector.bn_aggr(ln2_small[:, 0:2], ln2_raw[:, :]).then_inc(ln2_mean, 1)
                if g == 2 and ln_valid(b):
                    need(dve, ln2_rstd, b - 1)
                    nc.vector.tensor_scalar(xn2[:, :], x_sb[:, b - 2, :], ln2_small[:, 0:1], ln2_small[:, 3:4],
                                            ALU.subtract, ALU.mult).then_inc(ln2_norm, 1)
                if valid(b, g - 3):
                    i = (g - 3) % 2
                    need(dve, u_hi, s - 2)
                    nc.vector.scalar_tensor_tensor(out=u_ring[:, 1, i, :], in0=bank[3][:, :],
                                                   scalar=S_U / (S_C * S_P), in1=u_ring[:, 0, i, :],
                                                   op0=ALU.mult, op1=ALU.subtract).then_inc(u_lo, 1)
                if g == 1 and ln_valid(b):
                    need(dve, ln2_mean, b - 1)
                    nc.vector.tensor_scalar(ln2_small[:, 2:3], ln2_small[:, 1:2], EPS, None,
                                            ALU.add).then_inc(ln2_var, 1)
                if valid(b, g + 2):
                    need(dve, kt_hi, s + 3)
                    nc.vector.scalar_tensor_tensor(out=k_ring[:, 1, g % 2, :], in0=bank[2][:, :], scalar=S_K,
                                                   in1=k_ring[:, 0, g % 2, :], op0=ALU.mult,
                                                   op1=ALU.subtract).then_inc(kt_lo, 1)
                if valid(b, g + 3):
                    need(dve, k_squared, s + 4)
                    nc.vector.reduce_sum(kss[:, (g + 3) % 4, :], k_sq[:, :, :], AX_X).then_inc(k_summed, 1)
                if late_q_sums(b, g):
                    query_means(b, g)
                if g == 3 and valid(b, g - 4):
                    need(dve, out_proj, s - 3)
                    nc.vector.scalar_tensor_tensor(out=x_sb[:, b - 1, :], in0=bank[6][:, 0:DIM],
                                                   scalar=1.0 / (S_M * S_U), in1=x_sb[:, b - 1, :],
                                                   op0=ALU.mult, op1=ALU.add).then_inc(residual, 1)
                if valid(b, g + 3):
                    need(dve, k_summed, s + 4)
                    nc.vector.tensor_scalar(kms[:, (g + 3) % 4, :], kss[:, (g + 3) % 4, :], 1.0 / (D * k_c2),
                                            EPS / k_c2, ALU.mult, ALU.add).then_inc(k_meansq, 1)
                if code_valid(b):
                    c = b - 1
                    if g == 0:
                        if isinstance(b, int) and b == 1:
                            dve.wait_ge(codes_in, 16)
                        low = code_chunk(c).rearrange("p (n two) -> p n two", two=2)
                        nc.vector.tensor_copy(code16[:, :], low[:, :, 0]).then_inc(coded, 1)
                    elif g == 1:
                        need(dve, coded, c + 1)
                        signs(c, 0)
                        magnitude(c, 0)
                        join(c, 0)
                    elif g == 2:
                        signs(c, 1)
                        magnitude(c, 1)
                    else:
                        join(c, 1)
                if g == 0 and ln_valid(b):
                    c = b - 2
                    need(dve, sc_hi_done, c + 1)
                    if isinstance(b, int):
                        need(dve, decoded, c)
                    else:
                        dve.wait_ge(p_normed, s)
                    nc.vector.scalar_tensor_tensor(out=sc_lo[:, :], in0=scale_f[:, bass.ds(c * CW, CW)],
                                                   scalar=S_F * FP4_BIAS, in1=sc_hi[:, :], op0=ALU.mult,
                                                   op1=ALU.subtract).then_inc(sc_lo_done, 1)

            def keys_ahead(s):
                normalise_keys(s // NG, s % NG)

            def behind(s):
                if s == -3:
                    ln_low(0)
                    split("wk1")
                    keys_ahead(-2)
                if s == -2:
                    split("wq1")
                    keys_ahead(-1)
                    m_low(0)
                    m_low(1)
                    split("wk2")
                    ln_stats(1)
                if s == -1:
                    split("wk3")
                    keys_ahead(0)
                    m_low(2)
                    m_low(3)
                if s == 0:
                    m_low(4)
                    keys_ahead(1)
                    m_low(5)
                    split("cx_a")
                if s == 1:
                    m_low(6)
                    m_low(7)
                    keys_ahead(2)
                if s in (2, 4):
                    ln_stats(s // 2 + 1)
                if s == 2:
                    keys_ahead(3)
                if s == 3:
                    split("ct_b")
                if s == 5:
                    split("cx_b")
                if 1 <= s < B - 1:
                    ln_low(s)
                if s == NS + 2:
                    tile(0, 0, 0)
                if s == NS + 3:
                    tile(0, 0, 1)

            steps(dve, step, behind)

            def finish(half):
                for i in range(4):
                    dve.wait_ge(down, downs(half, 2 * CH * (half + 1) + i))
                    if half:
                        dve.wait_ge(out_done, 16 * 4)
                    nc.vector.scalar_tensor_tensor(out=y[:, DIM * i:DIM * i + DIM], in0=bank[SUM[i]][:, 0:DIM],
                                                   scalar=1.0 / (S_F * S_I), in1=x_sb[:, 4 * half + i, :],
                                                   op0=ALU.mult, op1=ALU.add).then_inc(y_done, 1)

            for g in range(3):
                step(B + 1, g)
            for half in range(2):
                if half:
                    tile(half, 0, 0)
                    tile(half, 0, 1)
                    tile(half, 1, 0)
                    tile(half, 1, 1)
                else:
                    tile(0, 1, 0)
                    hide(0, 1, 1)
                    ln2_low(B + 1)
                    hidden_low(0, 1, 1)
                with dve.Fori(2, CH) as c:
                    tile(half, c, 0)
                    tile(half, c, 1)
                finish(half)

        @block.tensor
        def _(pe):
            def three(dst, a, b, first=True, last=True):
                (a_hi, a_lo), (b_hi, b_lo) = a, b
                nc.tensor.matmul(dst, a_hi, b_hi, start=first, stop=False)
                nc.tensor.matmul(dst, a_hi, b_lo, start=False, stop=False)
                return nc.tensor.matmul(dst, a_lo, b_hi, start=False, stop=last)

            def ln_turn(n):
                dst, t = ln_view(n)
                tiles = range(t.start // T, t.stop // T)
                pe.wait_ge(ln_norm, tiles[-1] + 1)
                if n:
                    pe.wait_ge(q_meansq, n + 2)
                for k in range(KD):
                    for j, b in enumerate(tiles):
                        ins = nc.tensor.transpose(dst[:, k, T * j:T * j + T],
                                                  xn1[:, DIM * b + P * k:DIM * b + P * k + P], ident[:, :])
                ins.then_inc(ln_turned, 1)

            def m_product(i):
                if i >= 2:
                    pe.wait_ge(m_lo_done, i - 1)
                pe.wait_ge(w_in["wv"], 16)
                pe.wait_ge(w_in["wo0" if i < 4 else "wo1"], 16)
                for t in range(2):
                    h = 2 * i + t
                    ins = nc.tensor.matmul(bank[M_BANK[i]][:, DIM * t:DIM * t + DIM],
                                           wv_f[:, CD * h:CD * h + CD], wo_f[:, DIM * h:DIM * h + DIM],
                                           start=True, stop=True)
                ins.then_inc(m_prod, 1)

            def ln2_turn(b):
                need(pe, ln2_norm, b - 1)
                for k in range(KD):
                    ins = nc.tensor.transpose(ln2_view(b)[:, k, :],
                                              xn2[:, :].rearrange("p (f two) -> p two f", two=2)[:, k, :],
                                              ident[:, :])
                ins.then_inc(ln2_turned, 1)

            def gate_up_proj(half, c, i):
                u = 2 * (CH * half + c) + i
                need(pe, hidden, u - 1)
                for mat, dst in enumerate((GATE[i], UP[i])):
                    for k in range(KD):
                        w = bass.ds(c * 1536 + (768 * k + 256 * mat + P * i), P)
                        t = slice(HT * half, HT * half + HT)
                        ins = three(bank[dst][:, :], (wf_hi[:, w], wf_lo[:, w]),
                                    (xt_hi[:, k, t], xt_lo[:, k, t]), k == 0, k == KD - 1)
                ins.then_inc(gate_up, 1)

            pe.wait_ge(const_done, 1)

            def q_sums(b, g):
                if not valid(b, g + 1):
                    return
                s = NG * b + g
                need(pe, q_squared, s + 2)
                need(pe, q_meansq, s + 1)
                if g == 3 and ln_valid(b):
                    need(pe, ln2_lo, b - 1)
                if isinstance(b, int) and 2 <= s < B:
                    pe.wait_ge(ln_lo, s)
                for i in range(HG):
                    ins = nc.tensor.matmul(bank[7][:, i:i + 1], q_sq[:, T * i:T * i + T], ones[:, :],
                                           start=True, stop=True)
                ins.then_inc(q_sumsq, 1)

            def step(b, g):
                s = NG * b + g
                if isinstance(b, int) and NS <= s < NS + 2:
                    if s == NS:
                        pe.wait_ge(decoded, 1)
                        pe.wait_ge(ln2_lo, B // 2)
                        pe.wait_ge(q_lo, NS)
                    pe.wait_ge(exps, s - 1)
                    gate_up_proj(0, 0, s - NS)
                if valid(b, g):
                    need(pe, q_lo, s + 1)
                    need(pe, kt_lo, s + 1)
                    need(pe, exps, s - 1)
                    for i in range(HG):
                        c = slice(T * i, T * i + T)
                        ins = three(bank[g % 2][:, c], (q_ring[:, 0, g % 2, c], q_ring[:, 1, g % 2, c]),
                                    (k_ring[:, 0, g % 2, c], k_ring[:, 1, g % 2, c]))
                    ins.then_inc(scores, 1)
                if valid(b, g - 2):
                    need(pe, p_normed, s - 1)
                    if valid(b, g + 1):
                        need(pe, kt_lo, s + 2)
                    else:
                        need(pe, pt_lo, s - 2)
                    for i in range(HG):
                        c = slice(T * i, T * i + T)
                        ins = nc.tensor.transpose(bank[2][:, c], pn[:, (g - 2) % 2, c], ident[:, :])
                    ins.then_inc(p_turned, 1)
                if g == 3 and ln_valid(b):
                    if valid(b, g):
                        need(pe, q_meansq, s + 1)
                    ln2_turn(b)
                if isinstance(b, int) and s == 2 * NG - 1:
                    pe.wait_ge(lo_done["cx_b"], 1)
                if valid(b, g - 3):
                    need(pe, pt_lo, s - 2)
                    need(pe, u_lo, s - 3)
                    bb = b + (g - 3) // NG
                    c = bass.ds(bb * CD, CD)
                    i = (g - 3) % 2
                    if isinstance(b, int) and s == 3:
                        pe.wait_ge(lo_done["cx_a"], 1)
                        pe.wait_ge(m_lo_done, MG)
                    three(bank[3][:, :], (cx_hi[:, c], cx_lo[:, c]),
                          (pt_ring[:, 0, i, :], pt_ring[:, 1, i, :])).then_inc(mixed, 1)
                if valid(b, g - 4):
                    need(pe, u_lo, s - 3)
                    if g == 0:
                        need(pe, residual, b - 1)
                    for i in range(HG):
                        c = slice(T * i, T * i + T)
                        ins = three(bank[6][:, 0:DIM], (u_ring[:, 0, g % 2, c], u_ring[:, 1, g % 2, c]),
                                    (m_hi[:, HG * g + i, :], m_lo[:, HG * g + i, :]),
                                    g == 0 and i == 0, g == NG - 1 and i == HG - 1)
                    ins.then_inc(out_proj, 1)
                if not late_q_sums(b, g):
                    q_sums(b, g)
                if valid(b, g + 2):
                    need(pe, k_normed, s + 3)
                    if valid(b, g - 2):
                        need(pe, pt_lo, s - 1)
                    else:
                        need(pe, kt_lo, s + 2)
                    for i in range(HG):
                        c = slice(T * i, T * i + T)
                        ins = nc.tensor.transpose(bank[2][:, c], kn[:, g % 2, c], ident[:, :])
                    ins.then_inc(k_turned, 1)
                if valid(b, g + 3):
                    need(pe, k_normed, s + 3)
                    bb, gg = b + (g + 3) // NG, (g + 3) % NG
                    c = bass.ds(bb * T, T)
                    w = slice(512 * gg, 512 * gg + 512)
                    if isinstance(b, int) and (s < 1 or s == 2 * NG - 3):
                        if s == -3:
                            pe.wait_ge(lo_done["ct_a"], 1)
                        pe.wait_ge(lo_done[f"wk{gg}" if s < 1 else "ct_b"], 1)
                    three(bank[4][:, :], (ct_hi[:, c], ct_lo[:, c]),
                          (wk_hi[:, w], wk_lo[:, w])).then_inc(k_proj, 1)
                if isinstance(b, int) and -2 <= s < MG // 2 - 2:
                    m_product(2 * s + 4)
                    m_product(2 * s + 5)
                if late_q_sums(b, g):
                    q_sums(b, g)
                if valid(b, g + 2):
                    need(pe, q_lo, s + 2)
                    bb, gg = b + (g + 2) // NG, (g + 2) % NG
                    if isinstance(b, int) and s < 2:
                        pe.wait_ge(lo_done[f"wq{gg}"], 1)
                        pe.wait_ge(ln_lo, 1)
                    c = bass.ds(bb * T, T)
                    for i in range(HG):
                        w = slice(D * (HG * gg + i), D * (HG * gg + i) + D)
                        for k in range(KD):
                            ins = three(bank[5][:, T * i:T * i + T], (wq_hi[:, k, w], wq_lo[:, k, w]),
                                        (xt_hi[:, k, c], xt_lo[:, k, c]), k == 0, k == KD - 1)
                    ins.then_inc(q_proj, 1)

            def behind(s):
                if s == -3:
                    ln_turn(0)
                if 1 <= s < B - 1:
                    ln_turn(s)

            steps(pe, step, behind)

            def down_proj(half, c, i, first=False, last=False):
                u = 2 * (CH * half + c) + i
                need(pe, h_lo, u + 1)
                w = bass.ds(c * 1536 + (768 * i + 512), DIM)
                for t in range(4):
                    a = slice(P * t, P * t + P)
                    ins = three(bank[SUM[t]][:, 0:DIM], (pt_ring[:, 0, i, a], pt_ring[:, 1, i, a]),
                                (wf_hi[:, w], wf_lo[:, w]), first, last)
                    if last or t == 3:
                        ins.then_inc(down, 1)

            for half in range(2):
                def both(c, first=False):
                    if half == 0:
                        need(pe, decoded, c + 1)
                    for i in range(2):
                        gate_up_proj(half, c, i)
                        if first and i == 1 and half == 0:
                            pe.wait_ge(hidden, 3)
                            ln2_turn(B + 1)
                        if first and i == 0:
                            if half:
                                pe.wait_ge(y_done, 4)
                            else:
                                pe.wait_ge(pt_lo, NS)
                                pe.wait_ge(u_lo, NS)
                                pe.wait_ge(residual, B)
                                pe.wait_ge(ln2_lo, B - 1)
                        down_proj(half, c - 1, i, first=first and i == 0)

                if half:
                    gate_up_proj(half, 0, 0)
                    gate_up_proj(half, 0, 1)
                both(1, first=True)
                if half == 0:
                    pe.wait_ge(ln2_lo, B)
                with pe.Fori(2, CH) as c:
                    both(c)
                down_proj(half, CH - 1, 0)
                down_proj(half, CH - 1, 1, last=True)


def kernel(**inputs):
    import numpy as np
    import concourse.bacc as bacc
    from concourse.bass_utils import run_bass_kernel_spmd

    a = {n: np.asarray(v) for n, v in inputs.items()}

    def columns(w):
        return w.T.reshape(w.shape[1], CH, P, 2).transpose(0, 1, 3, 2).reshape(w.shape[1], CH, 2 * P)

    dp, ds = a["L0_ffn_down_W_packed"], a["L0_ffn_down_scales"]
    down_codes = dp.T.reshape(CH, P, DIM).transpose(1, 0, 2)
    down_scales = ds.T.reshape(CH, 2 * P // BLK, DIM).transpose(1, 0, 2)
    codes = np.stack([columns(a["L0_ffn_gate_W_packed"]), columns(a["L0_ffn_up_W_packed"]), down_codes], axis=2)
    scales = np.stack([columns(a["L0_ffn_gate_scales"]), columns(a["L0_ffn_up_scales"]), down_scales], axis=2)
    arrays = {
        "x": a["x"].reshape(B * T, DIM),
        "ctx": a["ctx_1024"].reshape(B * T, CD),
        "ctx_t": a["ctx_1024"].reshape(B * T, CD).T,
        "wq": a["L0_xattn_Wq"],
        "wk": a["L0_xattn_Wk"],
        "wv_t": a["L0_xattn_Wv"].reshape(CD, H, D).transpose(2, 1, 0).reshape(D, H * CD),
        "wo": a["L0_xattn_Wo"],
        "gq": a["L0_xattn_gq"].reshape(D, 1),
        "gk": a["L0_xattn_gk"].reshape(D, 1),
        "packed": codes.reshape(P, CH * 3 * DIM),
        "scales": scales.reshape(8, CH * 3 * DIM),
    }
    arrays = {n: np.ascontiguousarray(v) for n, v in arrays.items()}
    nc = bacc.Bacc("TRN2", target_bir_lowering=False, num_devices=1)
    args = [nc.dram_tensor(n, v.shape, mybir.dt.from_np(v.dtype), kind="ExternalInput").ap()
            for n, v in arrays.items()]
    out = nc.dram_tensor("out", (B * T, DIM), F32, kind="ExternalOutput").ap()
    xattn_ffn(nc, *args, out)
    r = run_bass_kernel_spmd(nc, [arrays], core_ids=[0])
    return r.results[0]["out"].reshape(B, T, DIM)
```
